# Optimizing a Trainium2 kernel written in Bass

```python
import numpy as np
import jax
import jax.numpy as jnp

def _softmax(x, axis=-1):
    return jax.nn.softmax(x, axis=axis)
def _gelu(x):
    return jax.nn.gelu(x, approximate=True)
def _silu(x):
    return jax.nn.silu(x)
def _sigmoid(x):
    return jax.nn.sigmoid(x)
def _layernorm(x, axis=-1, eps=1e-5):
    m = jnp.mean(x, axis=axis, keepdims=True)
    v = jnp.var(x, axis=axis, keepdims=True)
    return (x - m) / jnp.sqrt(v + eps)
def _scatter_add(tgt, idx, src, axis=0):
    return tgt.at[idx].add(src)
def _segment_sum(src, seg, n):
    return jax.ops.segment_sum(src, seg, n)

kernel_name = 'mk_conv_preact_d2_conv_nhwc128_50f380'

def setup_inputs(seed: int = 0):
    np.random.seed(seed)
    _w = jnp.asarray
    def _rec_inputs():
        import jax
        import jax.numpy as jnp
        _gk = jax.random.key(seed)
        x = 7.22e-05 + 1 * jax.random.normal(jax.random.fold_in(_gk, 1), (1, 256, 256, 128), jnp.float32)
        return x
    x = _rec_inputs()
    def _L0_conv_setup():
        import jax, jax.numpy as jnp
        import numpy as np
        B, N, DIM, H = (1, 256, 128, 4)
        key = jax.random.key(seed)
        ks = jax.random.split(key, 7)
        w = lambda k, shp: jax.random.normal(k, shp, dtype=jnp.float32) * 0.05
        return {'pair_repr': jax.random.normal(ks[0], (B, N, N, DIM), dtype=jnp.float32), 'Wq': w(ks[1], (DIM, DIM)), 'Wk': w(ks[2], (DIM, DIM)), 'Wv': w(ks[3], (DIM, DIM)), 'Wb': w(ks[4], (DIM, H)), 'Wo': w(ks[5], (DIM, DIM)), 'Wg': w(ks[6], (DIM, DIM))}
    _L0_conv_all = _L0_conv_setup()
    _L0_conv_in = {k: v for k, v in _L0_conv_all.items() if k in ('Wq', 'Wk', 'Wv', 'Wb', 'Wo', 'Wg', )}
    del _L0_conv_all

    def _L1_conv_setup():
        import jax, jax.numpy as jnp
        import numpy as np
        import math
        D_MODEL = 128
        D_STATE = 16
        D_CONV = 3
        EXPAND = 2
        D_INNER = EXPAND * D_MODEL
        DT_RANK = math.ceil(D_MODEL / 16)
        B, H, W = (2, 64, 64)
        LN_EPS = 1e-05

        def _local_scan(x, Hh, Ww, w_h, w_w, flip=False, column_first=False):
            Bb, C = (x.shape[0], x.shape[1])
            Hg, Wg = (Hh // w_h, Ww // w_w)
            x = x.reshape(Bb, C, Hg, w_h, Wg, w_w)
            if column_first:
                x = x.transpose(0, 1, 4, 2, 5, 3)
            else:
                x = x.transpose(0, 1, 2, 4, 3, 5)
            x = x.reshape(Bb, C, -1)
            if flip:
                x = x[:, :, ::-1]
            return x

        def _selective_scan(u, delta, A, Bm, Cm, D, delta_bias):
            Bsz, Dch, L = u.shape
            K, N = (Bm.shape[1], A.shape[1])
            d = Dch // K
            delta = jax.nn.softplus(delta + delta_bias[None, :, None])
            A4 = A.reshape(K, d, N)
            u4 = u.reshape(Bsz, K, d, L)
            dt4 = delta.reshape(Bsz, K, d, L)

            def step(h, inp):
                ut, dt, bt, ct = inp
                dA = jnp.exp(dt[..., None] * A4)
                h = dA * h + (dt * ut)[..., None] * bt[:, :, None, :]
                y = jnp.einsum('bkdn,bkn->bkd', h, ct)
                return (h, y)
            xs_t = (u4.transpose(3, 0, 1, 2), dt4.transpose(3, 0, 1, 2), Bm.transpose(3, 0, 1, 2), Cm.transpose(3, 0, 1, 2))
            h0 = jnp.zeros((Bsz, K, d, N), u.dtype)
            _, ys = jax.lax.scan(step, h0, xs_t)
            y = ys.transpose(1, 2, 3, 0).reshape(Bsz, Dch, L)
            return y + u * D[None, :, None]
        key = jax.random.key(seed)
        ks = jax.random.split(key, 8)
        x = jax.random.normal(ks[0], (B, H, W, D_MODEL), jnp.float32)
        W_in = jax.random.normal(ks[1], (2 * D_INNER, D_MODEL), jnp.float32) * D_MODEL ** (-0.5)
        conv_w = jax.random.normal(ks[2], (D_INNER, 1, D_CONV, D_CONV), jnp.float32) * (1.0 / D_CONV)
        conv_b = jnp.zeros((D_INNER,), jnp.float32)
        x_proj_w = jax.random.normal(ks[3], (4, DT_RANK + 2 * D_STATE, D_INNER), jnp.float32) * D_INNER ** (-0.5)
        std = DT_RANK ** (-0.5)
        dt_proj_w = jax.random.uniform(ks[4], (4, D_INNER, DT_RANK), jnp.float32, -std, std)
        dt = jnp.exp(jax.random.uniform(ks[5], (4, D_INNER), jnp.float32) * (math.log(0.1) - math.log(0.001)) + math.log(0.001))
        dt = jnp.maximum(dt, 0.0001)
        dt_proj_b = dt + jnp.log(-jnp.expm1(-dt))
        A_logs = jnp.log(jnp.tile(jnp.arange(1, D_STATE + 1, dtype=jnp.float32)[None, :], (4 * D_INNER, 1)))
        Ds = jnp.ones((4 * D_INNER,), jnp.float32)
        ln_w = jnp.ones((D_INNER,), jnp.float32)
        ln_b = jnp.zeros((D_INNER,), jnp.float32)
        W_out = jax.random.normal(ks[6], (D_MODEL, D_INNER), jnp.float32) * D_INNER ** (-0.5)
        return dict(x=x, W_in=W_in, conv_w=conv_w, conv_b=conv_b, x_proj_w=x_proj_w, dt_proj_w=dt_proj_w, dt_proj_b=dt_proj_b, A_logs=A_logs, Ds=Ds, ln_w=ln_w, ln_b=ln_b, W_out=W_out)
    _L1_conv_all = _L1_conv_setup()
    _L1_conv_in = {k: v for k, v in _L1_conv_all.items() if k in ('W_in', 'conv_w', 'conv_b', 'x_proj_w', 'dt_proj_w', 'dt_proj_b', 'A_logs', 'Ds', 'ln_w', 'ln_b', 'W_out', )}
    del _L1_conv_all

    return {
        "x": x,
        "L0_conv_Wq": _L0_conv_in["Wq"],
        "L0_conv_Wk": _L0_conv_in["Wk"],
        "L0_conv_Wv": _L0_conv_in["Wv"],
        "L0_conv_Wb": _L0_conv_in["Wb"],
        "L0_conv_Wo": _L0_conv_in["Wo"],
        "L0_conv_Wg": _L0_conv_in["Wg"],
        "L1_conv_W_in": _L1_conv_in["W_in"],
        "L1_conv_conv_w": _L1_conv_in["conv_w"],
        "L1_conv_conv_b": _L1_conv_in["conv_b"],
        "L1_conv_x_proj_w": _L1_conv_in["x_proj_w"],
        "L1_conv_dt_proj_w": _L1_conv_in["dt_proj_w"],
        "L1_conv_dt_proj_b": _L1_conv_in["dt_proj_b"],
        "L1_conv_A_logs": _L1_conv_in["A_logs"],
        "L1_conv_Ds": _L1_conv_in["Ds"],
        "L1_conv_ln_w": _L1_conv_in["ln_w"],
        "L1_conv_ln_b": _L1_conv_in["ln_b"],
        "L1_conv_W_out": _L1_conv_in["W_out"],
    }

def reference(x, L0_conv_Wq, L0_conv_Wk, L0_conv_Wv, L0_conv_Wb, L0_conv_Wo, L0_conv_Wg, L1_conv_W_in, L1_conv_conv_w, L1_conv_conv_b, L1_conv_x_proj_w, L1_conv_dt_proj_w, L1_conv_dt_proj_b, L1_conv_A_logs, L1_conv_Ds, L1_conv_ln_w, L1_conv_ln_b, L1_conv_W_out):
    import jax
    import jax.numpy as jnp
    def _L0_conv_ref(pair_repr, Wq, Wk, Wv, Wb, Wo, Wg):
        import jax, jax.numpy as jnp
        import numpy as np
        B, N, DIM, H = (1, 256, 128, 4)
        b, n, _, d = pair_repr.shape
        h = Wb.shape[1]
        hd = d // h
        scale = d ** (-0.5)
        q = (pair_repr @ Wq).reshape(b, n, n, h, hd)
        k = (pair_repr @ Wk).reshape(b, n, n, h, hd)
        v = (pair_repr @ Wv).reshape(b, n, n, h, hd)
        bias = pair_repr @ Wb
        scores = jnp.einsum('bnqhd,bnkhd->bnqkh', q, k) * scale + bias[:, None]
        weights = jax.nn.softmax(scores, axis=-2)
        out = jnp.einsum('bnqkh,bnkhd->bnqhd', weights, v).reshape(b, n, n, d)
        out = out @ Wo * jax.nn.sigmoid(pair_repr @ Wg)
        return out

    def _L1_conv_ref(x, W_in, conv_w, conv_b, x_proj_w, dt_proj_w, dt_proj_b, A_logs, Ds, ln_w, ln_b, W_out):
        import jax, jax.numpy as jnp
        import numpy as np
        import math
        D_MODEL = 128
        D_STATE = 16
        D_CONV = 3
        EXPAND = 2
        D_INNER = EXPAND * D_MODEL
        DT_RANK = math.ceil(D_MODEL / 16)
        B, H, W = (2, 64, 64)
        LN_EPS = 1e-05

        def _local_scan(x, Hh, Ww, w_h, w_w, flip=False, column_first=False):
            Bb, C = (x.shape[0], x.shape[1])
            Hg, Wg = (Hh // w_h, Ww // w_w)
            x = x.reshape(Bb, C, Hg, w_h, Wg, w_w)
            if column_first:
                x = x.transpose(0, 1, 4, 2, 5, 3)
            else:
                x = x.transpose(0, 1, 2, 4, 3, 5)
            x = x.reshape(Bb, C, -1)
            if flip:
                x = x[:, :, ::-1]
            return x

        def _selective_scan(u, delta, A, Bm, Cm, D, delta_bias):
            Bsz, Dch, L = u.shape
            K, N = (Bm.shape[1], A.shape[1])
            d = Dch // K
            delta = jax.nn.softplus(delta + delta_bias[None, :, None])
            A4 = A.reshape(K, d, N)
            u4 = u.reshape(Bsz, K, d, L)
            dt4 = delta.reshape(Bsz, K, d, L)

            def step(h, inp):
                ut, dt, bt, ct = inp
                dA = jnp.exp(dt[..., None] * A4)
                h = dA * h + (dt * ut)[..., None] * bt[:, :, None, :]
                y = jnp.einsum('bkdn,bkn->bkd', h, ct)
                return (h, y)
            xs_t = (u4.transpose(3, 0, 1, 2), dt4.transpose(3, 0, 1, 2), Bm.transpose(3, 0, 1, 2), Cm.transpose(3, 0, 1, 2))
            h0 = jnp.zeros((Bsz, K, d, N), u.dtype)
            _, ys = jax.lax.scan(step, h0, xs_t)
            y = ys.transpose(1, 2, 3, 0).reshape(Bsz, Dch, L)
            return y + u * D[None, :, None]
        Bb, Hh, Ww, _ = x.shape
        L = Hh * Ww
        d_inner = conv_b.shape[0]
        dt_rank = dt_proj_w.shape[2]
        N = A_logs.shape[1]
        xz = x @ W_in.T
        xc, z = jnp.split(xz, 2, axis=-1)
        xc = xc.transpose(0, 3, 1, 2)
        xc = jax.lax.conv_general_dilated(xc, conv_w, (1, 1), ((1, 1), (1, 1)), dimension_numbers=('NCHW', 'OIHW', 'NCHW'), feature_group_count=d_inner) + conv_b[None, :, None, None]
        xc = jax.nn.silu(xc)
        w_h, w_w = (Hh // 4, Ww // 4)
        x1 = _local_scan(xc, Hh, Ww, w_h, w_w)
        x2 = _local_scan(xc, Hh, Ww, w_h, w_w, column_first=True)
        x3 = _local_scan(xc, Hh, Ww, w_h, w_w, flip=True)
        x4 = _local_scan(xc, Hh, Ww, w_h, w_w, column_first=True, flip=True)
        xs = jnp.stack([x1, x2, x3, x4], axis=1)
        x_dbl = jnp.einsum('bkdl,kcd->bkcl', xs, x_proj_w)
        dts, Bs, Cs = jnp.split(x_dbl, [dt_rank, dt_rank + N], axis=2)
        dts = jnp.einsum('bkrl,kdr->bkdl', dts, dt_proj_w)
        u = xs.reshape(Bb, -1, L)
        delta = dts.reshape(Bb, -1, L)
        As = -jnp.exp(A_logs)
        out_y = _selective_scan(u, delta, As, Bs, Cs, Ds, dt_proj_b.reshape(-1)).reshape(Bb, 4, -1, L)
        inv_y = out_y[:, 2:4, :, ::-1]
        wh_y = out_y[:, 1].reshape(Bb, -1, Ww, Hh).transpose(0, 1, 3, 2).reshape(Bb, -1, L)
        invwh_y = inv_y[:, 1].reshape(Bb, -1, Ww, Hh).transpose(0, 1, 3, 2).reshape(Bb, -1, L)
        y = out_y[:, 0] + inv_y[:, 0] + wh_y + invwh_y
        y = y.transpose(0, 2, 1).reshape(Bb, Hh, Ww, -1)
        mu = jnp.mean(y, axis=-1, keepdims=True)
        var = jnp.mean(jnp.square(y - mu), axis=-1, keepdims=True)
        y = (y - mu) * jax.lax.rsqrt(var + LN_EPS) * ln_w + ln_b
        y = y * jax.nn.silu(z)
        return y @ W_out.T

    def _gn(v, G=32, eps=1e-5):
        B_, H_, W_, C_ = v.shape
        g = v.reshape(B_, H_, W_, G, C_ // G)
        m = jnp.mean(g, axis=(1, 2, 4), keepdims=True)
        s = jnp.var(g, axis=(1, 2, 4), keepdims=True)
        return ((g - m) / jnp.sqrt(s + eps)).reshape(v.shape)

    def _ln_c(v, eps=1e-6):
        m = jnp.mean(v, axis=-1, keepdims=True)
        s = jnp.var(v, axis=-1, keepdims=True)
        return (v - m) / jnp.sqrt(s + eps)

    def _ln_t(v, eps=1e-5):
        m = jnp.mean(v, axis=-1, keepdims=True)
        s = jnp.var(v, axis=-1, keepdims=True)
        return (v - m) / jnp.sqrt(s + eps)

    def _to_tokens(v):
        B_, H_, W_, C_ = v.shape
        return v.reshape(B_, H_ * W_, C_)
    def _from_tokens(t, like):
        return t.reshape(like.shape)

    x = x + _L0_conv_ref(_gn(x), L0_conv_Wq, L0_conv_Wk, L0_conv_Wv, L0_conv_Wb, L0_conv_Wo, L0_conv_Wg)
    x = x + _L1_conv_ref(_gn(x), L1_conv_W_in, L1_conv_conv_w, L1_conv_conv_b, L1_conv_x_proj_w, L1_conv_dt_proj_w, L1_conv_dt_proj_b, L1_conv_A_logs, L1_conv_Ds, L1_conv_ln_w, L1_conv_ln_b, L1_conv_W_out)
    return x


_drawn_inputs = setup_inputs


def setup_inputs(seed=0):
    import zlib

    import numpy as np

    out = dict(_drawn_inputs(seed))
    spreads = {'L1_conv_conv_b': (0.0, 0.289),
     'L1_conv_Ds': (1.0, 0.596),
     'L1_conv_ln_w': (1.0, 0.2),
     'L1_conv_ln_b': (0.0, 0.397)}
    factors = {'L0_conv_Wq': 8.0,
     'L0_conv_Wk': 8.0,
     'L0_conv_Wv': 3.908,
     'L0_conv_Wb': 7.76,
     'L0_conv_Wo': 3.924,
     'L0_conv_Wg': 8.0,
     'L1_conv_dt_proj_w': 4.664}
    for name, (base, spread) in spreads.items():
        noise = np.random.default_rng([zlib.crc32(name.encode()), seed]).standard_normal(out[name].shape)
        drawn = base * np.exp(spread * noise) if base else spread * noise
        out[name] = jnp.asarray(drawn.astype(out[name].dtype))
    for name, factor in factors.items():
        out[name] = (out[name] * factor).astype(out[name].dtype)
    return out
```

```python
import concourse.bass as bass
from concourse import mybir
from contextlib import ExitStack

F32, BF16 = mybir.dt.float32, mybir.dt.bfloat16
ALU, ACT, AX = mybir.AluOpType, mybir.ActivationFunctionType, mybir.AxisListType

P = 128
N, C = 256, 128
L = N * N
PAD = N + 2
GN_EPS = LN_EPS = 1e-5
HEADS, HD = 4, 32


class Phase(ExitStack):

    def __init__(self, nc, kept):
        super().__init__()
        self.nc, self.kept, self.semaphores = nc, kept, []

    def semaphore(self, name):
        self.semaphores.append(self.enter_context(self.nc.semaphore(name)))
        return self.semaphores[-1]

    def kept_semaphore(self, name):
        return self.kept.enter_context(self.nc.semaphore(name))

    def clear_semaphores(self):
        with self.nc.Block() as block:

            @block.sync
            def _(sp):
                for semaphore in self.semaphores:
                    sp.sem_clear(semaphore)


def run_phase(nc, kept, phase, *args):
    with Phase(nc, kept) as es:
        phase(nc, es, *args)
    es.clear_semaphores()


class Tile:

    def __init__(self, i, j, J):
        self.i, self.j, self.J = i, j, J

    def upto(self, per=1, plus=0):
        return self.i * (self.J * per) + (self.j * per + plus)

    def loads(self, room=0):
        return self.i * 16 + 16

    def moved(self, d):
        j = self.j + d
        return Tile(self.i + j // self.J, j % self.J, self.J)

    def number(self):
        return self.i * self.J + self.j if isinstance(self.i, int) else None


def wait(eng, semaphore, value):
    if not isinstance(value, int) or value > 0:
        eng.wait_ge(semaphore, value)


def for_tiles(eng, tiles, J, body):
    for j in range(J):
        body(Tile(0, j, J))
    with eng.Fori(1, tiles // J - 1) as i:
        for j in range(J):
            body(Tile(i, j, J))
    for j in range(J):
        body(Tile(tiles // J - 1, j, J))


def is_last(tile, tiles):
    return tile.number() == tiles - 1


def build_identity(pool, nc, ident, done, at):
    nc.gpsimd.memset(ident[:, :], 0.0).then_inc(done, 1)
    pool.wait_ge(done, at + 1)
    nc.gpsimd.affine_select(out=ident[:, :], in_=ident[:, :], compare_op=ALU.not_equal, fill=1.0,
                            base=0, pattern=[[-1, P]], channel_multiplier=1).then_inc(done, 1)


def transpose_phase(nc, es, x, xT_dram, stats, tag="tr"):
    T, J = 512, 4
    tiles = L // T
    Q = T // P
    sb = lambda name, shape: es.enter_context(nc.sbuf_tensor(f"{tag}_{name}", shape, F32))
    sem = lambda name: es.semaphore(f"{tag}_{name}")
    ident, xin, xT = sb("ident", [P, P]), sb("xin", [P, J, Q, C]), sb("xT", [P, J, T])
    t_ps = es.enter_context(nc.psum_tensor(f"{tag}_ps", [P, J, Q, P], F32))
    ident_built, transposed, copied, measured = sem("ident_built"), sem("transposed"), sem("copied"), sem("measured")
    x_loaded = [sem(f"x_loaded{j}") for j in range(J)]
    xT_stored = [es.kept_semaphore(f"{tag}_xT_stored{j}") for j in range(J)]
    block = es.enter_context(nc.Block())

    @block.sync
    def _(sp):
        def body(t):
            wait(sp, transposed, t.upto(1, 1 - J))
            sp.dma_start(xin[:, t.j, :, :],
                         x[bass.ds(t.upto(T), T), :].rearrange("(p q) c -> p q c", q=Q)).then_inc(x_loaded[t.j], 16)

        for_tiles(sp, tiles, J, body)

    @block.gpsimd
    def _(pool):
        build_identity(pool, nc, ident, ident_built, 0)

        def body(t):
            wait(pool, copied, t.upto(1, 1))
            pool.dma_start(xT_dram[:, bass.ds(t.upto(T), T)], xT[:, t.j, :]).then_inc(xT_stored[t.j], 16)

        for_tiles(pool, tiles, J, body)
        for j in range(J):
            pool.wait_ge(xT_stored[j], tiles // J * 16)

    @block.tensor
    def _(pe):
        pe.wait_ge(ident_built, 2)

        def body(t):
            wait(pe, x_loaded[t.j], t.loads())
            wait(pe, copied, t.upto(1, 1 - J))
            for q in range(Q):
                ins = nc.tensor.transpose(t_ps[:, t.j, q, :], xin[:, t.j, q, :], ident[:, :])
            ins.then_inc(transposed, 1)

        for_tiles(pe, tiles, J, body)

    @block.scalar
    def _(act):
        def body(t):
            wait(act, transposed, t.upto(1, 1))
            wait(act, xT_stored[t.j], t.loads() - 16)
            wait(act, measured, t.upto(1, 1 - J))
            nc.scalar.activation(xT[:, t.j, :].rearrange("c (p q) -> c q p", q=Q), t_ps[:, t.j, :, :],
                                 ACT.Copy).then_inc(copied, 1)

        for_tiles(act, tiles, J, body)

    @block.vector
    def _(dve):
        def body(t):
            wait(dve, copied, t.upto(1, 1))
            nc.vector.bn_stats(stats[:, bass.ds(t.upto(1), 1), :].rearrange("p a b -> p (a b)"), xT[:, t.j, :])\
              .then_inc(measured, 1)

        for_tiles(dve, tiles, J, body)


def norm_phase(nc, es, stats, mean, rstd, tag):
    G = 4
    sb = lambda name, shape: es.enter_context(nc.sbuf_tensor(f"{tag}_{name}", shape, F32))
    sem = lambda name: es.semaphore(f"{tag}_{name}")
    average, mv, moments = sb("average", [P, P]), sb("mv", [P, 2]), sb("moments", [P, 2])
    square, var = sb("square", [P, 1]), sb("var", [P, 1])
    m_ps = es.enter_context(nc.psum_tensor(f"{tag}_ps", [P, 2], F32))
    averager_built, step, averaged = sem("averager_built"), sem("step"), sem("averaged")
    root_taken = sem("root_taken")
    block = es.enter_context(nc.Block())

    @block.gpsimd
    def _(pool):
        view = average[:, :].rearrange("p (g j) -> p g j", j=G)
        nc.gpsimd.memset(average[:, :], 1.0 / G).then_inc(averager_built, 1)
        pool.wait_ge(averager_built, 1)
        nc.gpsimd.affine_select(out=view, in_=view, compare_op=ALU.is_ge, fill=0.0, base=0,
                                pattern=[[-G, P // G], [0, G]], channel_multiplier=1).then_inc(averager_built, 1)
        pool.wait_ge(averager_built, 2)
        nc.gpsimd.affine_select(out=view, in_=view, compare_op=ALU.is_ge, fill=0.0, base=G - 1,
                                pattern=[[G, P // G], [0, G]], channel_multiplier=-1).then_inc(averager_built, 1)

    @block.tensor
    def _(pe):
        pe.wait_ge(averager_built, 3)
        pe.wait_ge(step, 4)
        nc.tensor.matmul(m_ps[:, :], average[:, :], moments[:, :], start=True, stop=True).then_inc(averaged, 1)

    @block.vector
    def _(dve):
        made = [0]

        def chained(ins):
            made[0] += 1
            ins.then_inc(step, 1)
            dve.wait_ge(step, made[0])

        chained(nc.vector.bn_aggr(mv[:, :], stats[:, :, :]))
        chained(nc.vector.tensor_tensor(square[:, :], mv[:, 0:1], mv[:, 0:1], ALU.mult))
        chained(nc.vector.tensor_copy(moments[:, 0:1], mv[:, 0:1]))
        chained(nc.vector.tensor_tensor(moments[:, 1:2], mv[:, 1:2], square[:, :], ALU.add))
        dve.wait_ge(averaged, 1)
        chained(nc.vector.tensor_copy(mean[:, :], m_ps[:, 0:1]))
        chained(nc.vector.tensor_tensor(square[:, :], mean[:, :], mean[:, :], ALU.mult))
        chained(nc.vector.tensor_tensor(var[:, :], m_ps[:, 1:2], square[:, :], ALU.subtract))
        chained(nc.vector.tensor_scalar(var[:, :], var[:, :], GN_EPS, None, ALU.add))
        dve.wait_ge(root_taken, 1)
        chained(nc.vector.reciprocal(rstd[:, :], var[:, :]))

    @block.scalar
    def _(act):
        act.wait_ge(step, 8)
        nc.scalar.activation(var[:, :], var[:, :], ACT.Sqrt).then_inc(root_taken, 1)


def bias_phase(nc, es, xT_dram, mean, rstd, w_bias, bias_dram):
    T, J = 512, 4
    tiles = L // T
    sb = lambda name, shape: es.enter_context(nc.sbuf_tensor(f"bi_{name}", shape, F32))
    sem = lambda name: es.semaphore(f"bi_{name}")
    wb, xT, xn, out = sb("wb", [P, HEADS]), sb("xT", [P, J, T]), sb("xn", [P, J, T]), sb("out", [HEADS, J, T])
    b_ps = es.enter_context(nc.psum_tensor("bi_ps", [HEADS, J, T], F32))
    w_loaded, normed, projected, copied = sem("w_loaded"), sem("normed"), sem("projected"), sem("copied")
    x_loaded = [sem(f"x_loaded{j}") for j in range(J)]
    stored = [es.kept_semaphore(f"bi_stored{j}") for j in range(J)]
    block = es.enter_context(nc.Block())

    @block.sync
    def _(sp):
        sp.dma_start(wb[:, :], w_bias).then_inc(w_loaded, 16)

        def body(t):
            wait(sp, normed, t.upto(1, 1 - J))
            sp.dma_start(xT[:, t.j, :], xT_dram[:, bass.ds(t.upto(T), T)]).then_inc(x_loaded[t.j], 16)

        for_tiles(sp, tiles, J, body)

    @block.vector
    def _(dve):
        def body(t):
            wait(dve, x_loaded[t.j], t.loads())
            wait(dve, projected, t.upto(1, 1 - J))
            nc.vector.tensor_scalar(xn[:, t.j, :], xT[:, t.j, :], mean[:, :], rstd[:, :], ALU.subtract, ALU.mult)\
              .then_inc(normed, 1)

        for_tiles(dve, tiles, J, body)

    @block.tensor
    def _(pe):
        pe.wait_ge(w_loaded, 16)

        def body(t):
            wait(pe, normed, t.upto(1, 1))
            wait(pe, copied, t.upto(1, 1 - J))
            nc.tensor.matmul(b_ps[:, t.j, :], wb[:, :], xn[:, t.j, :], start=True, stop=True).then_inc(projected, 1)

        for_tiles(pe, tiles, J, body)

    @block.scalar
    def _(act):
        def body(t):
            wait(act, projected, t.upto(1, 1))
            wait(act, stored[t.j], t.loads() - 16)
            nc.scalar.activation(out[:, t.j, :], b_ps[:, t.j, :], ACT.Copy).then_inc(copied, 1)

        for_tiles(act, tiles, J, body)

    @block.gpsimd
    def _(pool):
        def body(t):
            wait(pool, copied, t.upto(1, 1))
            pool.dma_start(bias_dram[:, bass.ds(t.upto(T), T)], out[:, t.j, :]).then_inc(stored[t.j], 16)

        for_tiles(pool, tiles, J, body)
        for j in range(J):
            pool.wait_ge(stored[j], tiles // J * 16)


def attention_phase(nc, es, w, xT_dram, bias_dram, mean, rstd, x1_dram, stats):
    T, J = 2 * N, 2
    tiles, BLOCKS = L // T, 4
    KC = N // P
    SCALE = float(C) ** -0.5

    sb = lambda name, shape: es.enter_context(nc.sbuf_tensor(f"at_{name}", shape, F32))
    ps = lambda name, shape: es.enter_context(nc.psum_tensor(f"at_{name}", shape, F32))
    sem = lambda name: es.semaphore(f"at_{name}")

    ident = sb("ident", [P, P])
    wqkvg, wo = sb("wqkvg", [P, 4, C]), sb("wo", [P, C])
    bias = sb("bias", [P, KC, HEADS, N])
    xT, xn, xres = sb("xT", [P, J, T]), sb("xn", [P, J, T]), sb("xres", [P, J, T])
    q, k, v = sb("q", [P, J, T]), sb("k", [P, J, T]), sb("v", [P, J, T // P, C])
    gate = sb("gate", [P, J, T])
    S, E = sb("S", [P, 2, HEADS, N]), sb("E", [P, 2, HEADS, N])
    top, low = sb("top", [P, 4, HEADS]), sb("low", [P, 4, HEADS])
    total, inverse = sb("total", [P, 4, HEADS]), sb("inverse", [P, 4, HEADS])
    ET = sb("ET", [P, 2, HEADS, KC, P])
    O, OT = sb("O", [P, 2, C]), sb("OT", [P, T])
    gated = sb("gated", [P, T])
    x1 = sb("x1", [P, J, 2, PAD])
    margin = sb("margin", [P, PAD])

    S_ps, ET_ps = ps("S_ps", [P, HEADS, N]), ps("ET_ps", [P, HEADS, KC, P])
    pr_ps = ps("pr_ps", [P, 2, T])
    O_ps, OT_ps = ps("O_ps", [P, T]), ps("OT_ps", [P, T])

    ident_built, w_loaded, margin_stored, zeroed = (
        sem("ident_built"), sem("w_loaded"), sem("margin_stored"), sem("zeroed"))
    x_loaded, res_loaded, x1_stored = ([sem(f"{s}{j}") for j in range(J)]
                                       for s in ("x_loaded", "res_loaded", "x1_stored"))
    normed, q_made, k_made, g_made, v_made, out_made = map(
        sem, ("normed", "q_made", "k_made", "g_made", "v_made", "out_made"))
    q_copied, k_copied, g_exp, v_copied = map(sem, ("q_copied", "k_copied", "g_exp", "v_copied"))
    gate_step, gated_made, x1_made, measured = map(sem, ("gate_step", "gated_made", "x1_made", "measured"))
    half_scored, scored, biased, topped, lowered, exped = map(sem, ("half_scored", "scored", "biased", "topped", "lowered", "exped"))
    turned, ET_copied, inverted, weighed, O_made, O_turned, OT_copied = map(
        sem, ("turned", "ET_copied", "inverted", "weighed", "O_made", "O_turned", "OT_copied"))

    block = es.enter_context(nc.Block())

    def count(t, b):
        return t.upto(BLOCKS, b + 1)

    @block.sync
    def _(sp):
        for i, name in enumerate(("Wq", "Wk", "Wv", "Wg")):
            sp.dma_start(wqkvg[:, i, :], w[name]).then_inc(w_loaded, 16)
        sp.dma_start(wo[:, :], w["Wo"]).then_inc(w_loaded, 16)
        for qc in range(KC):
            sp.dma_start(bias[:, qc, :, :],
                         bias_dram.rearrange("h (c q k) -> q c h k", c=KC, k=N)[:, qc, :, :]).then_inc(w_loaded, 16)
        sp.wait_ge(zeroed, 2)
        for row in (0, PAD - 1):
            sp.dma_start(x1_dram[:, row, :], margin[:, :]).then_inc(margin_stored, 16)

        def load(t):
            wait(sp, normed, t.upto(1, 1 - J))
            sp.dma_start(xT[:, t.j, :], xT_dram[:, bass.ds(t.upto(T), T)]).then_inc(x_loaded[t.j], 16)

        def load_residual(t):
            wait(sp, x1_made, t.upto(1, 1 - J))
            sp.dma_start(xres[:, t.j, :], xT_dram[:, bass.ds(t.upto(T), T)]).then_inc(res_loaded[t.j], 16)

        def store(t):
            wait(sp, x1_made, t.upto(1, 1))
            sp.dma_start(x1_dram[:, bass.ds(t.upto(2, 1), 2), :], x1[:, t.j, :, :]).then_inc(x1_stored[t.j], 16)

        def body(t):
            load_residual(t)
            if not is_last(t, tiles):
                load(t.moved(1))
            if t.number() != 0:
                store(t.moved(-1))

        load(Tile(0, 0, J))
        for_tiles(sp, tiles, J, body)
        store(Tile(tiles // J - 1, J - 1, J))
        for j in range(J):
            sp.wait_ge(x1_stored[j], tiles // J * 16)
        sp.wait_ge(margin_stored, 2 * 16)

    @block.gpsimd
    def _(pool):
        build_identity(pool, nc, ident, ident_built, 0)
        nc.gpsimd.memset(margin[:, :], 0.0).then_inc(zeroed, 1)
        nc.gpsimd.memset(x1[:, :, :, :], 0.0).then_inc(zeroed, 1)

        def finish(t):
            wait(pool, gated_made, t.upto(1, 1))
            wait(pool, res_loaded[t.j], t.loads())
            wait(pool, x1_stored[t.j], t.loads() - 16)
            wait(pool, measured, t.upto(1, 1 - J))
            nc.gpsimd.tensor_tensor(x1[:, t.j, :, 1:N + 1], gated[:, :].rearrange("c (r p) -> c r p", r=2),
                                    xres[:, t.j, :].rearrange("c (r p) -> c r p", r=2), ALU.add).then_inc(x1_made, 1)

        def body(t):
            if t.number() != 0:
                finish(t.moved(-1))

        pool.wait_ge(zeroed, 2)
        for_tiles(pool, tiles, J, body)
        finish(Tile(tiles // J - 1, J - 1, J))

    @block.tensor
    def _(pe):
        pe.wait_ge(ident_built, 2)
        pe.wait_ge(w_loaded, 7 * 16)

        def project(t, which):
            if which == 0:
                wait(pe, normed, t.upto(1, 1))
                wait(pe, g_exp, t.upto(1, 0))
                nc.tensor.matmul(pr_ps[:, 0, :], wqkvg[:, 0, :], xn[:, t.j, :], start=True, stop=True)\
                  .then_inc(q_made, 1)
            elif which == 1:
                wait(pe, v_copied, t.upto(1, 0))
                nc.tensor.matmul(pr_ps[:, 1, :], wqkvg[:, 1, :], xn[:, t.j, :], start=True, stop=True)\
                  .then_inc(k_made, 1)
            elif which == 2:
                wait(pe, q_copied, t.upto(1, 1))
                wait(pe, gated_made, t.upto(1, -1))
                nc.tensor.matmul(pr_ps[:, 0, :], wqkvg[:, 3, :], xn[:, t.j, :], start=True, stop=True)\
                  .then_inc(g_made, 1)
            else:
                wait(pe, k_copied, t.upto(1, 1))
                for c in range(T // P):
                    ins = nc.tensor.matmul(pr_ps[:, 1, c * P:(c + 1) * P], xn[:, t.j, c * P:(c + 1) * P],
                                           wqkvg[:, 2, :], start=True, stop=True)
                ins.then_inc(v_made, 1)

        def score(t, b, part):
            row, qc = b // KC, b % KC
            if b == 0 and part == 0:
                wait(pe, q_copied, t.upto(1, 1))
                wait(pe, k_copied, t.upto(1, 1))
            if part == 0:
                wait(pe, biased, count(t, b - 1))
            else:
                wait(pe, half_scored, count(t, b))
            for h in (part, part + 2):
                rows = slice(h * HD, (h + 1) * HD)
                q0, k0 = row * N + qc * P, row * N
                ins = nc.tensor.matmul(S_ps[:, h, :], q[rows, t.j, q0:q0 + P], k[rows, t.j, k0:k0 + N],
                                       start=True, stop=True)
            ins.then_inc(scored if part else half_scored, 1)

        def turn(t, b):
            wait(pe, exped, count(t, b))
            wait(pe, ET_copied, count(t, b - 1))
            for h in range(HEADS):
                for kc in range(KC):
                    ins = nc.tensor.transpose(ET_ps[:, h, kc, :], E[:, b % 2, h, kc * P:(kc + 1) * P], ident[:, :])
            ins.then_inc(turned, 1)

        def weigh(t, b):
            if b == 0:
                wait(pe, v_copied, t.upto(1, 1))
            wait(pe, ET_copied, count(t, b))
            wait(pe, O_made, count(t, b - 1))
            for h in range(HEADS):
                for kc in range(KC):
                    ins = nc.tensor.matmul(O_ps[:, h * HD:(h + 1) * HD], ET[:, b % 2, h, kc, :],
                                           v[:, t.j, b // KC * KC + kc, h * HD:(h + 1) * HD],
                                           start=kc == 0, stop=kc == KC - 1)
            ins.then_inc(weighed, 1)

        def turn_out(t, b):
            wait(pe, O_made, count(t, b))
            if b == 0:
                wait(pe, OT_copied, t.upto(1, 0))
            nc.tensor.transpose(OT_ps[:, b * P:(b + 1) * P], O[:, b % 2, :], ident[:, :]).then_inc(O_turned, 1)

        def output(t, ahead):
            wait(pe, OT_copied, t.upto(1, 1))
            wait(pe, q_copied, t.upto(1, 1 + ahead))
            wait(pe, g_exp, t.upto(1, 1 + min(ahead, 1)))
            wait(pe, gated_made, t.upto(1, 0))
            nc.tensor.matmul(pr_ps[:, 0, :], wo[:, :], OT[:, :], start=True, stop=True).then_inc(out_made, 1)

        def body(t):
            after = None if is_last(t, tiles) else t.moved(1)
            before = None if t.number() == 0 else t.moved(-1)
            for b in range(BLOCKS):
                for which in {0: (0, 1), 1: (3,), 3: (2,)}.get(b, ()) if after else ():
                    project(after, which)
                ahead = (t, b + 1) if b < BLOCKS - 1 else (after, 0) if after else None
                if ahead:
                    score(*ahead, 0)
                if b >= 1:
                    weigh(t, b - 1)
                elif before:
                    weigh(before, BLOCKS - 1)
                if ahead:
                    score(*ahead, 1)
                if b >= 2:
                    turn_out(t, b - 2)
                elif before:
                    turn_out(before, b + BLOCKS - 2)
                turn(t, b)
                if b == 2 and before:
                    output(before, 2 if after else 1)

        first, last = Tile(0, 0, J), Tile(tiles // J - 1, J - 1, J)
        for which in range(4):
            project(first, which)
        score(first, 0, 0)
        score(first, 0, 1)
        for_tiles(pe, tiles, J, body)
        weigh(last, BLOCKS - 1)
        for b in (BLOCKS - 2, BLOCKS - 1):
            turn_out(last, b)
        output(last, 0)

    @block.scalar
    def _(act):
        act.preload_act_table_set("natural_log_exp_and_others")

        def copy_q(t):
            wait(act, q_made, t.upto(1, 1))
            wait(act, scored, count(t, 3 - 4 * J))
            nc.scalar.activation(q[:, t.j, :], pr_ps[:, 0, :], ACT.Copy, scale=SCALE).then_inc(q_copied, 1)

        def exp_g(t):
            wait(act, g_made, t.upto(1, 1))
            wait(act, gated_made, t.upto(1, 1 - J))
            nc.scalar.activation(gate[:, t.j, :], pr_ps[:, 0, :], ACT.Exp, scale=-1.0).then_inc(g_exp, 1)

        def exps(t, b):
            wait(act, lowered, count(t, b))
            wait(act, turned, count(t, b - 2))
            wait(act, inverted, count(t, b - 4))
            for h in range(HEADS):
                ins = nc.scalar.activation(E[:, b % 2, h, :], S[:, b % 2, h, :], ACT.Exp, bias=low[:, b, h:h + 1],
                                           accum_out=total[:, b, h:h + 1])
            ins.then_inc(exped, 1)

        def copy_ET(t, b):
            wait(act, turned, count(t, b))
            wait(act, weighed, count(t, b - 2))
            nc.scalar.activation(ET[:, b % 2, :, :, :], ET_ps[:, :, :, :], ACT.Copy).then_inc(ET_copied, 1)

        def copy_OT(t):
            wait(act, O_turned, count(t, 3))
            wait(act, out_made, t.upto(1, 0))
            nc.scalar.activation(OT[:, :], OT_ps[:, :], ACT.Copy).then_inc(OT_copied, 1)

        def body(t):
            after = None if is_last(t, tiles) else t.moved(1)
            before = None if t.number() == 0 else t.moved(-1)
            for b in range(BLOCKS):
                if b >= 1:
                    copy_ET(t, b - 1)
                elif before:
                    copy_ET(before, BLOCKS - 1)
                if after and b == 0:
                    copy_q(after)
                exps(t, b)
                if after and b == 3:
                    exp_g(after)
                if before and b == 1:
                    copy_OT(before)

        first, last = Tile(0, 0, J), Tile(tiles // J - 1, J - 1, J)
        copy_q(first)
        exp_g(first)
        for_tiles(act, tiles, J, body)
        copy_ET(last, BLOCKS - 1)
        copy_OT(last)

    @block.vector
    def _(dve):
        def norm(t):
            wait(dve, x_loaded[t.j], t.loads())
            wait(dve, v_made, t.upto(1, 1 - J))
            wait(dve, g_made, t.upto(1, 1 - J))
            nc.vector.tensor_scalar(xn[:, t.j, :], xT[:, t.j, :], mean[:, :], rstd[:, :], ALU.subtract, ALU.mult)\
              .then_inc(normed, 1)

        def copy_k(t):
            wait(dve, k_made, t.upto(1, 1))
            wait(dve, scored, count(t, 3 - 4 * J))
            nc.vector.tensor_copy(k[:, t.j, :], pr_ps[:, 1, :]).then_inc(k_copied, 1)

        def copy_v(t):
            wait(dve, v_made, t.upto(1, 1))
            wait(dve, weighed, count(t, 3 - 4 * J))
            nc.vector.tensor_copy(v[:, t.j, :, :], pr_ps[:, 1, :].rearrange("p (c d) -> p c d", d=C))\
              .then_inc(v_copied, 1)

        def make_gate(t, stage):
            if stage == 0:
                wait(dve, g_exp, t.upto(1, 1))
                nc.vector.tensor_scalar(gate[:, t.j, :], gate[:, t.j, :], 1.0, None, ALU.add).then_inc(gate_step, 1)
            else:
                wait(dve, gate_step, t.upto(2, 1))
                nc.vector.reciprocal(gate[:, t.j, :], gate[:, t.j, :]).then_inc(gate_step, 1)

        def maximum(t, b):
            wait(dve, scored, count(t, b))
            wait(dve, exped, count(t, b - 2))
            wait(dve, lowered, count(t, b - 4))
            nc.vector.tensor_tensor(S[:, b % 2, :, :], S_ps[:, :, :], bias[:, b % KC, :, :], ALU.add)\
              .then_inc(biased, 1)
            wait(dve, biased, count(t, b))
            nc.vector.tensor_reduce(top[:, b, :], S[:, b % 2, :, :], AX.X, ALU.max).then_inc(topped, 1)

        def negate(t, b):
            wait(dve, topped, count(t, b))
            nc.vector.tensor_scalar(low[:, b, :], top[:, b, :], -1.0, None, ALU.mult).then_inc(lowered, 1)

        def invert(t, b):
            wait(dve, exped, count(t, b))
            wait(dve, O_made, count(t, b - 4))
            nc.vector.reciprocal(inverse[:, b, :], total[:, b, :]).then_inc(inverted, 1)

        def make_O(t, b):
            wait(dve, weighed, count(t, b))
            wait(dve, inverted, count(t, b))
            wait(dve, O_turned, count(t, b - 2))
            nc.vector.tensor_tensor(O[:, b % 2, :].rearrange("p (h d) -> p h d", h=HEADS),
                                    O_ps[:, 0:C].rearrange("p (h d) -> p h d", h=HEADS),
                                    inverse[:, b, :].unsqueeze(2).to_broadcast([P, HEADS, HD]), ALU.mult)\
              .then_inc(O_made, 1)

        def make_gated(t):
            wait(dve, out_made, t.upto(1, 1))
            wait(dve, gate_step, t.upto(2, 2))
            wait(dve, x1_made, t.upto(1, 0))
            nc.vector.tensor_tensor(gated[:, :], pr_ps[:, 0, :], gate[:, t.j, :], ALU.mult).then_inc(gated_made, 1)

        def measure(t):
            wait(dve, x1_made, t.upto(1, 1))
            nc.vector.bn_stats(stats[:, bass.ds(t.upto(1), 1), :].rearrange("p a b -> p (a b)"),
                               x1[:, t.j, :, 1:N + 1]).then_inc(measured, 1)

        def body(t):
            after = None if is_last(t, tiles) else t.moved(1)
            before = None if t.number() == 0 else t.moved(-1)
            for b in range(BLOCKS):
                if after and b == 0:
                    norm(after)
                    copy_k(after)
                if b >= 1:
                    invert(t, b - 1)
                elif before:
                    invert(before, BLOCKS - 1)
                if after and b == 1:
                    copy_v(after)
                if b < BLOCKS - 1:
                    maximum(t, b + 1)
                    negate(t, b + 1)
                elif after:
                    maximum(after, 0)
                    negate(after, 0)
                if b >= 1:
                    make_O(t, b - 1)
                elif before:
                    make_O(before, BLOCKS - 1)
                if b < 2:
                    make_gate(t, b)
                if before and b == 2:
                    make_gated(before)
                if before and b == 3:
                    measure(before)

        first, last = Tile(0, 0, J), Tile(tiles // J - 1, J - 1, J)
        norm(first)
        copy_k(first)
        copy_v(first)
        maximum(first, 0)
        negate(first, 0)
        for_tiles(dve, tiles, J, body)
        invert(last, BLOCKS - 1)
        make_O(last, BLOCKS - 1)
        make_gated(last)
        measure(last)


WIN = 64
SIDE = N // WIN


class Window:

    def __init__(self, wy, v, j):
        self.wy, self.v, self.j = wy, v, j

    def upto(self, per=1, plus=0):
        return self.wy * (SIDE * per) + self.v * (2 * per) + (self.j * per + plus)

    def turns(self, per=1, plus=0):
        return self.wy * (SIDE // 2 * per) + self.v * per + plus

    def wx(self, per):
        return self.v * (2 * per) + self.j * per


def for_windows(eng, body):
    with eng.Fori(0, SIDE) as wy:
        with eng.Fori(0, SIDE // 2) as v:
            body(Window(wy, v, 0))
            body(Window(wy, v, 1))


def conv_phase(nc, es, w, x1_dram, mean, rstd, u_dram):
    TAPS, HALVES, ROWS = 9, 2, 8
    CHUNKS, BANKS = WIN // ROWS, 8
    sb = lambda name, shape: es.enter_context(nc.sbuf_tensor(f"cv_{name}", shape, F32))
    sem = lambda name: es.semaphore(f"cv_{name}")
    win, taps = sb("win", [P, 2 * P]), sb("taps", [P, TAPS, 2 * P])
    wt = sb("wt", [P, TAPS, 2 * P])
    cb = sb("cb", [P, HALVES])
    inside = sb("inside", [P, SIDE * SIDE, 4])
    patch = sb("patch", [P, 2, WIN + 2, WIN + 2])
    raw = sb("raw", [P, WIN + 2, WIN + 2])
    us = sb("us", [P, HALVES, WIN, WIN])
    uc = sb("uc", [P, HALVES, WIN, WIN])
    c_ps = es.enter_context(nc.psum_tensor("cv_ps", [P, BANKS, ROWS * WIN], F32))
    w_loaded, w_made, masks_made, raw_loaded = map(sem, ("w_loaded", "w_made", "masks_made", "raw_loaded"))
    normed, edge = map(sem, ("normed", "edge"))
    summed = [sem(f"summed{j}") for j in range(2)]
    activated = [sem(f"activated{b}") for b in range(BANKS)]
    turned = [sem(f"turned{h}") for h in range(HALVES)]
    us_stored, uc_stored = ([es.kept_semaphore(f"cv_{s}_stored{h}") for h in range(HALVES)] for s in ("us", "uc"))
    block = es.enter_context(nc.Block())
    UNITS = CHUNKS * HALVES

    @block.sync
    def _(sp):
        sp.dma_start(win[:, :], w["W_in"][:, 0:2 * P]).then_inc(w_loaded, 16)
        sp.dma_start(taps[:, :, :].rearrange("p t d -> p (t d)"),
                     w["conv_w"].partition_broadcast(P)).then_inc(w_loaded, 16)
        sp.dma_start(cb[:, :], w["conv_b"]).then_inc(w_loaded, 16)

        def body(t):
            sp.wait_ge(normed, t.upto())
            sp.dma_start(raw[:, :, :], x1_dram[:, bass.ds(t.wy * WIN, WIN + 2), bass.ds(t.wx(WIN), WIN + 2)])\
              .then_inc(raw_loaded, 16)

        for_windows(sp, body)

    @block.gpsimd
    def _(pool):
        def body(t):
            rows_at = t.wy * (SIDE * WIN * WIN) + t.wx(WIN * WIN)
            columns_at = t.wx(SIDE * WIN * WIN) + t.wy * (WIN * WIN)
            for half in range(HALVES):
                pool.wait_ge(activated[BANKS - 1], t.upto(HALVES, half + 1))
                pool.dma_start(u_dram[0, half][:, bass.ds(rows_at, WIN * WIN)],
                               us[:, half, :, :].rearrange("p a b -> p (a b)")).then_inc(us_stored[half], 16)
                pool.wait_ge(turned[half], t.upto(1, 1))
                pool.dma_start(u_dram[1, half][:, bass.ds(columns_at, WIN * WIN)],
                               uc[:, half, :, :].rearrange("p a b -> p (a b)")).then_inc(uc_stored[half], 16)

        for_windows(pool, body)
        for half in range(HALVES):
            pool.wait_ge(us_stored[half], SIDE * SIDE * 16)
            pool.wait_ge(uc_stored[half], SIDE * SIDE * 16)

    @block.vector
    def _(dve):
        nc.vector.memset(inside[:, :, :], 1.0).then_inc(masks_made, 1)
        edges = inside[:, :, :].rearrange("p (y x) e -> p y x e", x=SIDE)
        views = (edges[:, :, 0, 0], edges[:, :, SIDE - 1, 1], edges[:, 0, :, 2], edges[:, SIDE - 1, :, 3])
        dve.wait_ge(masks_made, 1)
        for view in views:
            nc.vector.memset(view, 0.0).then_inc(masks_made, 1)
        dve.wait_ge(w_loaded, 3 * 16)
        for tap in range(TAPS):
            ins = nc.vector.tensor_tensor(wt[:, tap, :], win[:, :], taps[:, tap, :], ALU.mult)
        ins.then_inc(w_made, 1)
        dve.wait_ge(masks_made, 5)

        def norm(t):
            dve.wait_ge(raw_loaded, t.upto(16, 16))
            dve.wait_ge(summed[t.j], t.turns(UNITS))
            nc.vector.tensor_scalar(patch[:, t.j, :, :], raw[:, :, :], mean[:, :], rstd[:, :], ALU.subtract, ALU.mult)\
              .then_inc(normed, 1)
            dve.wait_ge(normed, t.upto(1, 1))
            for e, view in enumerate((patch[:, t.j, :, 0:1], patch[:, t.j, :, WIN + 1:], patch[:, t.j, 0:1, :],
                                      patch[:, t.j, WIN + 1:, :])):
                dve.wait_ge(edge, t.upto(4, e))
                nc.vector.tensor_scalar(view, view, inside[:, bass.ds(t.upto(), 1), e], None, ALU.mult)\
                  .then_inc(edge, 1)

        def turn(t, half):
            dve.wait_ge(activated[BANKS - 1], t.upto(HALVES, half + 1))
            dve.wait_ge(uc_stored[half], t.upto(16))
            nc.vector.tensor_copy(uc[:, half, :, :], us[:, half, :, :].rearrange("p a b -> p b a"))\
              .then_inc(turned[half], 1)

        def body(t):
            norm(t)
            for half in range(HALVES):
                turn(t, half)

        for_windows(dve, body)

    @block.tensor
    def _(pe):
        pe.wait_ge(w_made, 1)

        def body(t):
            pe.wait_ge(edge, t.upto(4, 4))
            for half in range(HALVES):
                for c in range(CHUNKS):
                    pe.wait_ge(activated[c], t.upto(HALVES, half))
                    for tap in range(TAPS):
                        dy, dx = tap // 3, tap % 3
                        ins = nc.tensor.matmul(c_ps[:, c, :], wt[:, tap, half * P:(half + 1) * P],
                                               patch[:, t.j, c * ROWS + dy:(c + 1) * ROWS + dy, dx:dx + WIN],
                                               start=tap == 0, stop=tap == TAPS - 1)
                    ins.then_inc(summed[t.j], 1)

        for_windows(pe, body)

    @block.scalar
    def _(act):
        act.preload_act_table(ACT.Silu)
        act.wait_ge(w_loaded, 3 * 16)

        def body(t):
            for half in range(HALVES):
                act.wait_ge(us_stored[half], t.upto(16))
                act.wait_ge(turned[half], t.upto())
                for c in range(CHUNKS):
                    act.wait_ge(summed[t.j], t.turns(UNITS, half * CHUNKS + c + 1))
                    nc.scalar.activation(us[:, half, c * ROWS:(c + 1) * ROWS, :].rearrange("p a b -> p (a b)"),
                                         c_ps[:, c, :], ACT.Silu, bias=cb[:, half:half + 1])\
                      .then_inc(activated[c], 1)

        for_windows(act, body)


def scan_phase(nc, es, w, u_dram, y_dram, L):
    NS, R, DIRS, T = 16, 8, 4, 512
    NT = L // T
    NB, NU = 4, 4
    LAG = 2
    DT0 = 32
    PARTS = (0, 64, 96)

    def sb(name, shape, dt=F32):
        return es.enter_context(nc.sbuf_tensor("sc_" + name, shape, dt))

    def ps(name, shape):
        return es.enter_context(nc.psum_tensor("sc_" + name, shape, F32))

    def sem(name):
        return es.semaphore("sc_" + name)

    u = sb("u", [P, 2, 2, T])
    dt = sb("dt", [P, 2, 2, T])
    du = sb("du", [P, 2, 2, T])
    pre = sb("pre", [P, 2, T])
    spl = sb("spl", [P, 2, T])
    bc = sb("bc", [P, 2, T], BF16)
    rest = sb("rest", [P, T])
    dts = sb("dts", [DT0 + R, T])
    ROW, SEAM, SPAN = 2 * (T + 1), T, 2 * T + 1
    h = sb("h", [P, NS, ROW])
    dA = sb("dA", [P, NB, ROW])
    dBu = sb("dBu", [P, NU, ROW])
    yp = sb("yp", [P, 2, 2, T])
    Cb = sb("Cb", [P, NB, T])
    hC = sb("hC", [P, NB, 2, T])
    yo = sb("yo", [P, 2, 2, T])
    sel = sb("sel", [P, 2 * NS, P], BF16)
    ident = sb("ident", [P, P])
    xp = sb("xp", [P, DIRS, 2, P])
    dtw = sb("dtw", [DT0 + R, DIRS, 2, P])
    dtb = sb("dtb", [P, DIRS, 2])
    Dk = sb("Dk", [P, DIRS, 2])
    A = sb("A", [P, DIRS, 2, NS])
    xd_ps, dt_ps = ps("xd_ps", [P, T]), ps("dt_ps", [P, T])
    B_ps, C_ps, y_ps = ps("B_ps", [P, 2, T]), ps("C_ps", [P, 2, T]), ps("y_ps", [P, 2, T])

    weights_zeroed, weights_loaded = sem("weights_zeroed"), sem("weights_loaded")
    selectors_built, A_built = sem("selectors_built"), sem("A_built")
    u_loaded = [sem(f"u_loaded{j}") for j in range(2)]
    yp_loaded = [sem(f"yp_loaded{j}") for j in range(2)]
    y_stored = [sem(f"y_stored{j}") for j in range(2)]
    xd_made, dtraw_made = sem("xd_made"), sem("dtraw_made")
    high_made, mid_made, low_made = sem("high_made"), sem("mid_made"), sem("low_made")
    rest1_made, rest2_made = sem("rest1_made"), sem("rest2_made")
    pre_made, softplus_step = sem("pre_made"), sem("softplus_step")
    dt_made, du_made = sem("dt_made"), sem("du_made")
    B_made, C_made, y_summed = sem("B_made"), sem("C_made"), sem("y_summed")
    dA_made, Cb_made = sem("dA_made"), sem("Cb_made")
    seam_zeroed, h_zeroed, dBu_made, scanned = sem("seam_zeroed"), sem("h_zeroed"), sem("dBu_made"), sem("scanned")
    hC_made, yo_made = sem("hC_made"), sem("yo_made")

    def wait(eng, semaphore, value):
        if not isinstance(value, int) or value > 0:
            eng.wait_ge(semaphore, value)

    class Tile:

        def __init__(self, k, i, j):
            self.k, self.i, self.j = k, i, j

        def tiles(self, per=1, plus=0):
            return self.i * (2 * per) + ((self.k * NT + self.j) * per + plus)

        def loads(self):
            return self.i * 16 + (self.k * NT // 2 + 1) * 16

        def at(self):
            if self.k >= 2:
                return self.i * (-2 * T) + (NT - 1 - self.j) * T
            return self.i * (2 * T) + self.j * T

        def next(self):
            if self.j == 0:
                return Tile(self.k, self.i, 1)
            if isinstance(self.i, int) and self.i == NT // 2 - 1:
                return Tile(self.k + 1, 0, 0) if self.k + 1 < DIRS else None
            return Tile(self.k, self.i + 1, 0)

        def before(self):
            if self.j == 1:
                return Tile(self.k, self.i, 0)
            if isinstance(self.i, int) and self.i == 0:
                return Tile(self.k - 1, NT // 2 - 1, 1) if self.k else None
            return Tile(self.k, self.i - 1, 1)

        def order(self):
            return self.k % 2

        def first(self):
            return isinstance(self.i, int) and self.i == 0 and self.j == 0

    def for_tiles(eng, body):
        for k in range(DIRS):
            body(Tile(k, 0, 0))
            body(Tile(k, 0, 1))
            with eng.Fori(1, NT // 2 - 1) as i:
                body(Tile(k, i, 0))
                body(Tile(k, i, 1))
            body(Tile(k, NT // 2 - 1, 0))
            body(Tile(k, NT // 2 - 1, 1))

    def run(row, tile):
        return row[:, 0:SPAN][:, ::-1] if tile.k >= 2 else row[:, 0:SPAN]

    def halves(row):
        return row.rearrange("p (s t) -> p s t", s=2)[:, :, 0:T]

    def last_states(tile):
        return (T + 1, 0) if tile.k >= 2 else (T - 1, 2 * T)

    def both(ap):
        return ap.unsqueeze(1).to_broadcast([P, 2, T])

    block = es.enter_context(nc.Block())
    WEIGHT_DMAS = (len(PARTS) + 1) * 2 * DIRS + 4

    @block.sync
    def _(sp):
        sp.wait_ge(weights_zeroed, 1)
        for k in range(DIRS):
            for half in range(2):
                rows = w["x_proj"][k, half * P:(half + 1) * P, :]
                for part in PARTS:
                    sp.dma_start(xp[:, k, half, part:part + 2 * NS], rows[:, R:]).then_inc(weights_loaded, 16)
                sp.dma_start(xp[:, k, half, DT0:DT0 + R], rows[:, 0:R]).then_inc(weights_loaded, 16)
        sp.dma_start(dtw[DT0:DT0 + R, :, :, :], w["dt_w"]).then_inc(weights_loaded, 16)
        for here, there in ((dtb, w["dt_b"]), (Dk, w["D"]), (A, w["A_log"])):
            sp.dma_start(here[:], there).then_inc(weights_loaded, 16)

        def load_u(tile):
            sp.dma_start(u[:, tile.j, :, :],
                         u_dram[tile.order()].rearrange("s p l -> p s l")[:, :, bass.ds(tile.at(), T)])\
              .then_inc(u_loaded[tile.j], 16)

        def load_yp(tile):
            if tile.k < 2:
                return
            if tile.first():
                for j in range(2):
                    sp.wait_ge(y_stored[j], (tile.k - 1) * NT // 2 * 16)
            sp.dma_start(yp[:, tile.j, :, :],
                         y_dram[tile.k - 2].rearrange("s p l -> p s l")[:, :, bass.ds(tile.at(), T)])\
              .then_inc(yp_loaded[tile.j], 16)

        def store_y(tile):
            sp.dma_start(y_dram[tile.k].rearrange("s p l -> p s l")[:, :, bass.ds(tile.at(), T)],
                         yo[:, tile.j, :, :]).then_inc(y_stored[tile.j], 16)

        def body(tile):
            wait(sp, yo_made, tile.tiles())
            if tile.next():
                load_u(tile.next())
                load_yp(tile.next())
            if tile.before():
                store_y(tile.before())

        load_u(Tile(0, 0, 0))
        for_tiles(sp, body)
        last = Tile(DIRS - 1, NT // 2 - 1, 1)
        sp.wait_ge(yo_made, DIRS * NT)
        store_y(last)
        for j in range(2):
            sp.wait_ge(y_stored[j], DIRS * NT // 2 * 16)

    @block.gpsimd
    def _(pool):
        nc.gpsimd.memset(xp[:, :, :, :], 0.0).then_inc(weights_zeroed, 1)
        nc.gpsimd.memset(ident[:, :], 0.0).then_inc(selectors_built, 1)
        nc.gpsimd.memset(sel[:, :, :], 0.0).then_inc(selectors_built, 1)
        pool.wait_ge(selectors_built, 2)
        nc.gpsimd.affine_select(out=ident[:, :], in_=ident[:, :], compare_op=ALU.not_equal, fill=1.0,
                                base=0, pattern=[[-1, P]], channel_multiplier=1).then_inc(selectors_built, 1)
        for n, part in enumerate(PARTS):
            pool.wait_ge(selectors_built, 3 + n)
            nc.gpsimd.affine_select(out=sel[:, :, :], in_=sel[:, :, :], compare_op=ALU.not_equal, fill=1.0,
                                    base=-part, pattern=[[-1, 2 * NS], [0, P]], channel_multiplier=1)\
              .then_inc(selectors_built, 1)

        def make_du(tile):
            wait(pool, dt_made, tile.tiles(1, 1))
            wait(pool, dBu_made, tile.tiles(NS, -NS))
            wait(pool, u_loaded[tile.j], tile.loads())
            nc.gpsimd.tensor_tensor(du[:, tile.j, :, :], dt[:, tile.j, :, :], u[:, tile.j, :, :], ALU.mult)\
              .then_inc(du_made, 1)

        def body(tile):
            for n in range(NS):
                wait(pool, scanned, tile.tiles(NS, n + 1))
                wait(pool, Cb_made, tile.tiles(NS, n + 1))
                wait(pool, y_summed, tile.tiles(NS, n + 1 - NB))
                nc.gpsimd.tensor_tensor(hC[:, n % NB, :, :], halves(h[:, n, :]), both(Cb[:, n % NB, :]), ALU.mult)\
                  .then_inc(hC_made, 1)
                if n == 13 and tile.next():
                    make_du(tile.next())

        make_du(Tile(0, 0, 0))
        for_tiles(pool, body)

    @block.scalar
    def _(act):
        act.preload_act_table_set("natural_log_exp_and_others")
        act.wait_ge(weights_loaded, WEIGHT_DMAS * 16)
        nc.scalar.activation(A[:, :, :, :], A[:, :, :, :], ACT.Exp).then_inc(A_built, 1)
        act.wait_ge(A_built, 1)
        nc.scalar.mul(A[:, :, :, :], A[:, :, :, :], -1.0).then_inc(A_built, 1)
        act.wait_ge(A_built, 2)

        def high(tile):
            wait(act, xd_made, tile.tiles(1, 1))
            wait(act, C_made, tile.tiles(NS, -NS))
            wait(act, low_made, tile.tiles(1, 0))
            wait(act, dtraw_made, tile.tiles(2, 0))
            nc.scalar.activation(bc[:, tile.j, :], xd_ps[:, :], ACT.Copy)
            nc.scalar.activation(dts[DT0:DT0 + R, :], xd_ps[DT0:DT0 + R, :], ACT.Copy).then_inc(high_made, 1)

        def middle(tile):
            wait(act, rest1_made, tile.tiles(1, 1))
            nc.scalar.activation(bc[64:P, tile.j, :], rest[64:P, :], ACT.Copy).then_inc(mid_made, 1)

        def low(tile):
            wait(act, rest2_made, tile.tiles(1, 1))
            nc.scalar.activation(bc[96:P, tile.j, :], rest[96:P, :], ACT.Copy).then_inc(low_made, 1)

        def add_bias(tile, half):
            wait(act, dtraw_made, tile.tiles(2, half + 1))
            wait(act, dt_made, tile.tiles(1, 0))
            nc.scalar.activation(pre[:, half, :], dt_ps[:, :], ACT.Identity,
                                 bias=dtb[:, tile.k, half:half + 1]).then_inc(pre_made, 1)

        def softplus(tile, stage):
            if stage == 0:
                wait(act, pre_made, tile.tiles(2, 2))
                wait(act, dt_made, tile.tiles(1, 0))
                nc.scalar.activation(spl[:, :, :], pre[:, :, :], ACT.Abs).then_inc(softplus_step, 1)
            elif stage == 1:
                wait(act, softplus_step, tile.tiles(3, 1))
                nc.scalar.activation(spl[:, :, :], spl[:, :, :], ACT.Exp, scale=-1.0).then_inc(softplus_step, 1)
            else:
                wait(act, softplus_step, tile.tiles(3, 2))
                nc.scalar.activation(spl[:, :, :], spl[:, :, :], ACT.Ln, bias=1.0).then_inc(softplus_step, 1)

        front = {5: (high,), 7: (middle, lambda t: add_bias(t, 0)), 9: (lambda t: add_bias(t, 1), low),
                 10: (lambda t: softplus(t, 0),), 11: (lambda t: softplus(t, 1),), 12: (lambda t: softplus(t, 2),)}

        def whole_front(tile):
            for piece in (high, middle, low):
                piece(tile)
            for half in range(2):
                add_bias(tile, half)
            for stage in range(3):
                softplus(tile, stage)

        def decay(tile, n):
            if n == 0:
                wait(act, dt_made, tile.tiles(1, 1))
            wait(act, scanned, tile.tiles(NS, n + 1 - NB))
            if tile.first():
                act.wait_ge(h_zeroed, 2 * tile.k + 2)
            seam_state = last_states(tile)[1]
            nc.scalar.activation(dBu[:, n % NU, SEAM:SEAM + 1], h[:, n, seam_state:seam_state + 1], ACT.Copy)
            for half in range(2):
                ins = nc.scalar.activation(halves(dA[:, n % NB, :])[:, half, :], dt[:, tile.j, half, :], ACT.Exp,
                                           scale=A[:, tile.k, half, n:n + 1])
            ins.then_inc(dA_made, 1)

        def copy_C(tile, n):
            wait(act, C_made, tile.tiles(NS, n + 1))
            wait(act, hC_made, tile.tiles(NS, n + 1 - NB))
            nc.scalar.activation(Cb[:, n % NB, :], C_ps[:, n % 2, :], ACT.Copy).then_inc(Cb_made, 1)

        def body(tile):
            for n in range(NS):
                if n + 1 < NS:
                    decay(tile, n + 1)
                copy_C(tile, n)
                for piece in front.get(n, ()) if tile.next() else ():
                    piece(tile.next())
                if n == NS - 1 and tile.next():
                    decay(tile.next(), 0)

        whole_front(Tile(0, 0, 0))
        decay(Tile(0, 0, 0), 0)
        for_tiles(act, body)

    @block.vector
    def _(dve):
        def rest1(tile):
            wait(dve, high_made, tile.tiles(1, 1))
            wait(dve, low_made, tile.tiles(1, 0))
            nc.vector.tensor_tensor(rest[64:P, :], xd_ps[64:P, :], bc[64:P, tile.j, :], ALU.subtract)\
              .then_inc(rest1_made, 1)

        def rest2(tile):
            wait(dve, mid_made, tile.tiles(1, 1))
            nc.vector.tensor_tensor(rest[96:P, :], rest[96:P, :], bc[96:P, tile.j, :], ALU.subtract)\
              .then_inc(rest2_made, 1)

        def make_dt(tile):
            wait(dve, softplus_step, tile.tiles(3, 3))
            wait(dve, dA_made, tile.tiles(NS, -NS))
            nc.vector.scalar_tensor_tensor(out=dt[:, tile.j, :, :], in0=pre[:, :, :], scalar=0.0,
                                           in1=spl[:, :, :], op0=ALU.max, op1=ALU.add).then_inc(dt_made, 1)

        def make_dBu(tile, n):
            wait(dve, B_made, tile.tiles(NS, n + 1))
            wait(dve, scanned, tile.tiles(NS, n + 1 - NU))
            nc.vector.tensor_tensor(halves(dBu[:, n % NU, :]), du[:, tile.j, :, :], both(B_ps[:, n % 2, :]), ALU.mult)\
              .then_inc(dBu_made, 1)

        def finish_y(tile):
            wait(dve, y_summed, tile.tiles(NS, NS))
            wait(dve, y_stored[tile.j], tile.loads() - 16)
            for half in range(2):
                ins = nc.vector.scalar_tensor_tensor(
                    out=yo[:, tile.j, half, :], in0=u[:, tile.j, half, :], scalar=Dk[:, tile.k, half:half + 1],
                    in1=y_ps[:, half, :], op0=ALU.mult, op1=ALU.add)
            ins.then_inc(yo_made, 1)

        front = {6: rest1, 8: rest2, 13: make_dt}

        def body(tile):
            start = last_states(tile)[0]
            if tile.first():
                wait(dve, hC_made, tile.tiles(NS, 0))
                for state in last_states(tile):
                    nc.vector.memset(h[:, :, state:state + 1], 0.0).then_inc(h_zeroed, 1)
                dve.wait_ge(h_zeroed, 2 * tile.k + 2)
            for n in range(NS):
                if n + 1 < NS:
                    make_dBu(tile, n + 1)
                wait(dve, dA_made, tile.tiles(NS, n + 1))
                wait(dve, dBu_made, tile.tiles(NS, n + 1))
                wait(dve, hC_made, tile.tiles(NS, n + 1 - NS))
                nc.vector.tensor_tensor_scan(run(h[:, n, :], tile), run(dA[:, n % NB, :], tile),
                                             run(dBu[:, n % NU, :], tile), h[:, n, start:start + 1],
                                             ALU.mult, ALU.add).then_inc(scanned, 1)
                if n == 1 and tile.before():
                    finish_y(tile.before())
                if tile.next() and n in front:
                    front[n](tile.next())
                if n == NS - 1 and tile.next():
                    wait(dve, du_made, tile.next().tiles(1, 1))
                    make_dBu(tile.next(), 0)

        nc.vector.memset(dA[:, :, SEAM:SEAM + 1], 0.0).then_inc(seam_zeroed, 1)
        dve.wait_ge(seam_zeroed, 1)
        for piece in (rest1, rest2, make_dt):
            piece(Tile(0, 0, 0))
        dve.wait_ge(du_made, 1)
        make_dBu(Tile(0, 0, 0), 0)
        for_tiles(dve, body)
        finish_y(Tile(DIRS - 1, NT // 2 - 1, 1))

    @block.tensor
    def _(pe):
        pe.wait_ge(weights_loaded, WEIGHT_DMAS * 16)
        pe.wait_ge(selectors_built, 6)

        def project(tile, half):
            if half == 0:
                wait(pe, u_loaded[tile.j], tile.loads())
                wait(pe, high_made, tile.tiles(1, 0))
                wait(pe, rest1_made, tile.tiles(1, 0))
            ins = nc.tensor.matmul(xd_ps[:, :], xp[:, tile.k, half, :], u[:, tile.j, half, :],
                                   start=half == 0, stop=half == 1)
            if half == 1:
                ins.then_inc(xd_made, 1)

        def raw_dt(tile, half):
            wait(pe, high_made, tile.tiles(1, 1))
            wait(pe, pre_made, tile.tiles(2, half))
            nc.tensor.matmul(dt_ps[:, :], dtw[DT0:DT0 + R, tile.k, half, :], dts[DT0:DT0 + R, :],
                             start=True, stop=True).then_inc(dtraw_made, 1)

        def spread_B(tile, n):
            if n == 0:
                wait(pe, low_made, tile.tiles(1, 1))
            wait(pe, dBu_made, tile.tiles(NS, n - 1))
            nc.tensor.matmul(B_ps[:, n % 2, :], sel[:, n, :], bc[:, tile.j, :], start=True, stop=True)\
              .then_inc(B_made, 1)

        def spread_C(tile, n):
            wait(pe, Cb_made, tile.tiles(NS, n - 1))
            nc.tensor.matmul(C_ps[:, n % 2, :], sel[:, NS + n, :], bc[:, tile.j, :], start=True, stop=True)\
              .then_inc(C_made, 1)

        def add_before(tile, half):
            wait(pe, yp_loaded[tile.j], tile.loads() - NT * 16)
            nc.tensor.matmul(y_ps[:, half, :], ident[:, :], yp[:, tile.j, half, :], start=False, stop=False)

        def add_step(tile, n):
            if n == 0:
                wait(pe, yo_made, tile.tiles(1, 0))
            wait(pe, hC_made, tile.tiles(NS, n + 1))
            for half in range(2):
                ins = nc.tensor.matmul(y_ps[:, half, :], ident[:, :], hC[:, n % NB, half, :],
                                       start=n == 0, stop=n == NS - 1)
            ins.then_inc(y_summed, 1)

        def body(tile):
            for n in range(NS):
                if n + 2 < NS:
                    spread_B(tile, n + 2)
                elif tile.next():
                    spread_B(tile.next(), n + 2 - NS)
                if n + 1 < NS:
                    spread_C(tile, n + 1)
                elif tile.next():
                    spread_C(tile.next(), 0)
                if tile.next():
                    if n in (4, 5):
                        project(tile.next(), n - 4)
                    if n in (7, 9):
                        raw_dt(tile.next(), (n - 7) // 2)
                if n in (10, 11) and tile.k >= 2:
                    add_before(tile, n - 10)
                if n >= LAG:
                    add_step(tile, n - LAG)
                elif tile.before():
                    add_step(tile.before(), n - LAG + NS)

        for half in range(2):
            project(Tile(0, 0, 0), half)
        for half in range(2):
            raw_dt(Tile(0, 0, 0), half)
        for n in range(2):
            spread_B(Tile(0, 0, 0), n)
        spread_C(Tile(0, 0, 0), 0)
        for_tiles(pe, body)
        for n in range(NS - LAG, NS):
            add_step(Tile(DIRS - 1, NT // 2 - 1, 1), n)


def output_phase(nc, es, w, x1_dram, mean, rstd, y_rows, y_columns, out):
    HALVES, ROWS = 2, 8
    CHUNKS, T = WIN // ROWS, ROWS * WIN
    Q = T // P
    sb = lambda name, shape: es.enter_context(nc.sbuf_tensor(f"ou_{name}", shape, F32))
    ps = lambda name, shape: es.enter_context(nc.psum_tensor(f"ou_{name}", shape, F32))
    sem = lambda name: es.semaphore(f"ou_{name}")
    pair = lambda name: [sem(f"{name}{b}") for b in range(2)]

    ident, mean_of = sb("ident", [P, P]), sb("mean_of", [P, P])
    wz, wout = sb("wz", [P, 2 * P]), sb("wout", [P, HALVES, C])
    ln_w, ln_b = sb("ln_w", [P, HALVES]), sb("ln_b", [P, HALVES])
    w_scaled, w_shift = sb("w_scaled", [P, HALVES, C]), sb("w_shift", [P, HALVES, C])
    yb = sb("yb", [P, 2, HALVES, WIN, WIN])
    ya, x1 = sb("ya", [P, 2, HALVES, T]), sb("x1", [P, 2, T])
    y, yc, sq = sb("y", [P, 2, HALVES, T]), sb("yc", [P, 2, HALVES, T]), sb("sq", [P, 2, HALVES, T])
    xn, sz, ysz = sb("xn", [P, 2, T]), sb("sz", [P, 2, HALVES, T]), sb("ysz", [P, 2, HALVES, T])
    var, r = sb("var", [P, 2, Q]), sb("r", [P, 2, Q])
    power = sb("power", [P, Q])
    scaled, res = sb("scaled", [P, 2, Q, C]), sb("res", [P, 2, Q, C])
    mean_ps, z_ps = ps("mean_ps", [P, T]), ps("z_ps", [P, HALVES, T])
    var_ps = ps("var_ps", [P, T])
    main_ps, side_ps = ps("main_ps", [P, 2, Q, C]), ps("side_ps", [P, 2, Q, C])

    built, w_loaded, w_made = sem("built"), sem("w_loaded"), sem("w_made")
    ya_loaded, yb_loaded, x1_loaded = map(pair, ("ya_loaded", "yb_loaded", "x1_loaded"))
    stored = [es.kept_semaphore(f"ou_stored{b}") for b in range(2)]
    y_made, mean_made, yc_made, sq_made, var_made, var_copied, r_made = map(
        pair, ("y_made", "mean_made", "yc_made", "sq_made", "var_made", "var_copied", "r_made"))
    xn_made, z_made, sz_made, ysz_made, main_made, side_made, scaled_made, res_made = map(
        pair, ("xn_made", "z_made", "sz_made", "ysz_made", "main_made", "side_made", "scaled_made", "res_made"))
    block = es.enter_context(nc.Block())

    class Chunk:
        def __init__(self, t, c):
            self.t, self.c, self.b = t, c, c % 2

        def turns(self, per=1, plus=0):
            return self.t.upto(CHUNKS // 2 * per, self.c // 2 * per + plus)

        def other(self):
            return self.t.upto(CHUNKS // 2, (self.c + 1) // 2)

    def for_chunks(eng, stages):
        with eng.Fori(0, SIDE) as wy:
            with eng.Fori(0, SIDE // 2) as v:
                chunks = [Chunk(Window(wy, v, j), c) for j in range(2) for c in range(CHUNKS)]
                for s in range(len(chunks) + max(lag for lag, _ in stages)):
                    for lag, stage in stages:
                        if 0 <= s - lag < len(chunks):
                            stage(chunks[s - lag])

    def halves(ap):
        return ap.unsqueeze(1).to_broadcast([P, HALVES, T])

    @block.sync
    def _(sp):
        sp.dma_start(wz[:, :], w["W_in"][:, 2 * P:4 * P]).then_inc(w_loaded, 16)
        sp.dma_start(wout[:, :, :], w["W_out"].rearrange("(s p) c -> p s c", s=HALVES)).then_inc(w_loaded, 16)
        sp.dma_start(ln_w[:, :], w["ln_w"]).then_inc(w_loaded, 16)
        sp.dma_start(ln_b[:, :], w["ln_b"]).then_inc(w_loaded, 16)

        def load(k):
            t, c, b = k.t, k.c, k.b
            y0, x0 = t.wy * WIN + c * ROWS, t.wx(WIN)
            if c == 0:
                sp.wait_ge(y_made[1], t.turns(CHUNKS))
                for half in range(HALVES):
                    sp.dma_start(yb[:, t.j, half, :, :],
                                 y_columns[half].rearrange("p (x y) -> p x y", y=N)
                                 [:, bass.ds(x0, WIN), bass.ds(t.wy * WIN, WIN)]).then_inc(yb_loaded[t.j], 16)
            sp.wait_ge(y_made[b], k.turns())
            for half in range(HALVES):
                sp.dma_start(ya[:, b, half, :].rearrange("p (y x) -> p y x", x=WIN),
                             y_rows[half].rearrange("p (y x) -> p y x", x=N)
                             [:, bass.ds(y0, ROWS), bass.ds(x0, WIN)]).then_inc(ya_loaded[b], 16)
            sp.wait_ge(side_made[b], k.turns())
            sp.wait_ge(xn_made[b], k.turns())
            sp.dma_start(x1[:, b, :].rearrange("p (y x) -> p y x", x=WIN),
                         x1_dram[:, bass.ds(y0 + 1, ROWS), bass.ds(x0 + 1, WIN)]).then_inc(x1_loaded[b], 16)

        for_chunks(sp, [(0, load)])

    @block.gpsimd
    def _(pool):
        build_identity(pool, nc, ident, built, 0)
        nc.gpsimd.memset(mean_of[:, :], 1.0 / (2 * P)).then_inc(built, 1)
        nc.gpsimd.memset(power[:, :], -0.5).then_inc(built, 1)
        pool.wait_ge(built, 4)

        def add_y(k):
            t, c, b = k.t, k.c, k.b
            if c == 0:
                pool.wait_ge(yb_loaded[t.j], t.turns(HALVES * 16, HALVES * 16))
            pool.wait_ge(ya_loaded[b], k.turns(HALVES * 16, HALVES * 16))
            pool.wait_ge(mean_made[b], k.turns())
            pool.wait_ge(yc_made[b], k.turns())
            for half in range(HALVES):
                ins = nc.gpsimd.tensor_tensor(
                    y[:, b, half, :].rearrange("p (y x) -> p y x", x=WIN),
                    ya[:, b, half, :].rearrange("p (y x) -> p y x", x=WIN),
                    yb[:, t.j, half, :, c * ROWS:(c + 1) * ROWS].rearrange("p x y -> p y x"), ALU.add)
            ins.then_inc(y_made[b], 1)

        def make_r(k):
            b = k.b
            pool.wait_ge(var_copied[b], k.turns(1, 1))
            pool.wait_ge(scaled_made[b], k.turns())
            nc.gpsimd.tensor_tensor(r[:, b, :], var[:, b, :], power[:, :], ALU.pow).then_inc(r_made[b], 1)

        def store(k):
            t, c, b = k.t, k.c, k.b
            pool.wait_ge(res_made[b], k.turns(1, 1))
            for row in range(2):
                pool.dma_start(
                    out.rearrange("(y r) x c -> r x y c", r=2)
                    [row, bass.ds(t.wx(WIN), WIN), bass.ds(t.wy * (WIN // 2) + c * (ROWS // 2), Q), :],
                    res[row * WIN:(row + 1) * WIN, b, :, :]).then_inc(stored[b], 16)

        for_chunks(pool, [(0, add_y), (2, make_r), (3, store)])
        for b in range(2):
            pool.wait_ge(stored[b], SIDE * SIDE * CHUNKS // 2 * 2 * 16)

    @block.tensor
    def _(pe):
        pe.wait_ge(built, 4)
        pe.wait_ge(w_made, 4)

        def take_mean(k):
            b = k.b
            pe.wait_ge(y_made[b], k.turns(1, 1))
            pe.wait_ge(yc_made[1 - b], k.other())
            for half in range(HALVES):
                ins = nc.tensor.matmul(mean_ps[:, :], mean_of[:, :], y[:, b, half, :], start=half == 0, stop=half == 1)
            ins.then_inc(mean_made[b], 1)

        def take_z(k):
            b = k.b
            pe.wait_ge(xn_made[b], k.turns(1, 1))
            pe.wait_ge(sz_made[1 - b], k.other())
            for half in range(HALVES):
                ins = nc.tensor.matmul(z_ps[:, half, :], wz[:, half * P:(half + 1) * P], xn[:, b, :],
                                       start=True, stop=True)
            ins.then_inc(z_made[b], 1)

        def columns(ap, q):
            return ap[:, q * P:(q + 1) * P]

        def take_var(k):
            b = k.b
            pe.wait_ge(sq_made[b], k.turns(1, 1))
            pe.wait_ge(var_copied[1 - b], k.other())
            for q in range(Q):
                for half in range(HALVES):
                    ins = nc.tensor.matmul(var_ps[:, q:q + 1], columns(sq[:, b, half, :], q), mean_of[:, 0:1],
                                           start=half == 0, stop=half == 1)
            ins.then_inc(var_made[b], 1)

        def side(k):
            b = k.b
            pe.wait_ge(sz_made[b], k.turns(1, 1))
            pe.wait_ge(x1_loaded[b], k.turns(16, 16))
            pe.wait_ge(res_made[b], k.turns())
            for q in range(Q):
                nc.tensor.matmul(side_ps[:, b, q, :], columns(x1[:, b, :], q), ident[:, :], start=True, stop=False)
                for half in range(HALVES):
                    ins = nc.tensor.matmul(side_ps[:, b, q, :], columns(sz[:, b, half, :], q), w_shift[:, half, :],
                                           start=False, stop=half == 1)
            ins.then_inc(side_made[b], 1)

        def main(k):
            b = k.b
            pe.wait_ge(ysz_made[b], k.turns(1, 1))
            pe.wait_ge(scaled_made[b], k.turns())
            for q in range(Q):
                for half in range(HALVES):
                    ins = nc.tensor.matmul(main_ps[:, b, q, :], columns(ysz[:, b, half, :], q), w_scaled[:, half, :],
                                           start=half == 0, stop=half == 1)
            ins.then_inc(main_made[b], 1)

        for_chunks(pe, [(0, take_z), (0, take_mean), (1, side), (1, take_var), (1, main)])

    @block.scalar
    def _(act):
        act.preload_act_table(ACT.Silu)

        def silu(k):
            b = k.b
            act.wait_ge(z_made[b], k.turns(1, 1))
            act.wait_ge(side_made[b], k.turns())
            act.wait_ge(ysz_made[b], k.turns())
            nc.scalar.activation(sz[:, b, :, :], z_ps[:, :, :], ACT.Silu).then_inc(sz_made[b], 1)

        def square(k):
            b = k.b
            act.wait_ge(yc_made[b], k.turns(1, 1))
            act.wait_ge(var_made[b], k.turns())
            nc.scalar.activation(sq[:, b, :, :], yc[:, b, :, :], ACT.Square).then_inc(sq_made[b], 1)

        for_chunks(act, [(0, silu), (0, square)])

    @block.vector
    def _(dve):
        dve.wait_ge(w_loaded, 4 * 16)
        for half in range(HALVES):
            nc.vector.tensor_scalar(w_scaled[:, half, :], wout[:, half, :], ln_w[:, half:half + 1], None, ALU.mult)\
              .then_inc(w_made, 1)
            nc.vector.tensor_scalar(w_shift[:, half, :], wout[:, half, :], ln_b[:, half:half + 1], None, ALU.mult)\
              .then_inc(w_made, 1)

        def norm_x(k):
            b = k.b
            dve.wait_ge(x1_loaded[b], k.turns(16, 16))
            dve.wait_ge(z_made[b], k.turns())
            nc.vector.tensor_scalar(xn[:, b, :], x1[:, b, :], mean[:, :], rstd[:, :], ALU.subtract, ALU.mult)\
              .then_inc(xn_made[b], 1)

        def center(k):
            b = k.b
            dve.wait_ge(mean_made[b], k.turns(1, 1))
            dve.wait_ge(sq_made[b], k.turns())
            dve.wait_ge(ysz_made[b], k.turns())
            nc.vector.tensor_tensor(yc[:, b, :, :], y[:, b, :, :], halves(mean_ps[:, :]), ALU.subtract)\
              .then_inc(yc_made[b], 1)

        def gate(k):
            b = k.b
            dve.wait_ge(sz_made[b], k.turns(1, 1))
            dve.wait_ge(yc_made[b], k.turns(1, 1))
            dve.wait_ge(main_made[b], k.turns())
            nc.vector.tensor_tensor(ysz[:, b, :, :], yc[:, b, :, :], sz[:, b, :, :], ALU.mult).then_inc(ysz_made[b], 1)

        def copy_var(k):
            b = k.b
            dve.wait_ge(var_made[b], k.turns(1, 1))
            dve.wait_ge(r_made[b], k.turns())
            nc.vector.tensor_scalar(var[:, b, :], var_ps[:, 0:Q], LN_EPS, None, ALU.add).then_inc(var_copied[b], 1)

        def finish(k):
            b = k.b
            dve.wait_ge(main_made[b], k.turns(1, 1))
            dve.wait_ge(r_made[b], k.turns(1, 1))
            dve.wait_ge(res_made[b], k.turns())
            nc.vector.tensor_tensor(scaled[:, b, :, :], main_ps[:, b, :, :],
                                    r[:, b, :].unsqueeze(2).to_broadcast([P, Q, C]), ALU.mult)\
              .then_inc(scaled_made[b], 1)
            dve.wait_ge(side_made[b], k.turns(1, 1))
            dve.wait_ge(scaled_made[b], k.turns(1, 1))
            dve.wait_ge(stored[b], k.turns(2 * 16))
            nc.vector.tensor_tensor(res[:, b, :, :], scaled[:, b, :, :], side_ps[:, b, :, :], ALU.add)\
              .then_inc(res_made[b], 1)

        for_chunks(dve, [(0, norm_x), (1, center), (1, gate), (2, copy_var), (3, finish)])


def build_program(nc, x, w, out):
    dram = lambda name, shape: nc.dram_tensor(name, shape, F32, kind="Internal").ap()
    xT = dram("xT_scratch", (C, L))
    bias = dram("bias_scratch", (HEADS, L))
    x1 = dram("x1_scratch", (C, PAD, PAD))
    u = dram("u_scratch", (2, 2, P, L))
    y = dram("y_scratch", (4, 2, P, L))
    with ExitStack() as kept:
        sb = lambda name, shape: kept.enter_context(nc.sbuf_tensor(name, shape, F32))
        stats = sb("stats", [P, L // 512, 6])
        mean_x, rstd_x, mean_x1, rstd_x1 = (sb(name, [P, 1]) for name in ("mean_x", "rstd_x", "mean_x1", "rstd_x1"))
        run_phase(nc, kept, transpose_phase, x.rearrange("b y x c -> (b y x) c"), xT, stats)
        run_phase(nc, kept, norm_phase, stats, mean_x, rstd_x, "nx")
        run_phase(nc, kept, bias_phase, xT, mean_x, rstd_x, w["Wb"], bias)
        run_phase(nc, kept, attention_phase, w, xT, bias, mean_x, rstd_x, x1, stats)
        run_phase(nc, kept, norm_phase, stats, mean_x1, rstd_x1, "n1")
        run_phase(nc, kept, conv_phase, w, x1, mean_x1, rstd_x1, u)
        run_phase(nc, kept, scan_phase, w, u, y, L)
        run_phase(nc, kept, output_phase, w, x1, mean_x1, rstd_x1, y[2], y[3], out.rearrange("b y x c -> (b y) x c"))


def kernel(**inputs):
    import numpy as np
    import concourse.bacc as bacc
    from concourse import mybir as my
    from concourse.bass_utils import run_bass_kernel_spmd

    given = {name: np.asarray(a) for name, a in inputs.items()}
    conv = {name.removeprefix("L1_conv_"): a for name, a in given.items() if name.startswith("L1_conv_")}
    laid = {name: given["L0_conv_" + name] for name in ("Wq", "Wk", "Wv", "Wb", "Wo", "Wg")}
    laid |= {
        "W_in": conv["W_in"].T,
        "conv_w": conv["conv_w"].reshape(2 * P, 9).T.reshape(-1),
        "conv_b": conv["conv_b"].reshape(2, P).T,
        "x_proj": conv["x_proj_w"].transpose(0, 2, 1),
        "dt_w": conv["dt_proj_w"].transpose(2, 0, 1).reshape(8, 4, 2, P),
        "dt_b": conv["dt_proj_b"].reshape(4, 2, P).transpose(2, 0, 1),
        "D": conv["Ds"].reshape(4, 2, P).transpose(2, 0, 1),
        "A_log": conv["A_logs"].reshape(4, 2, P, 16).transpose(2, 0, 1, 3),
        "ln_w": conv["ln_w"].reshape(2, P).T,
        "ln_b": conv["ln_b"].reshape(2, P).T,
        "W_out": conv["W_out"].T,
    }
    arrays = {"in_x": np.ascontiguousarray(given["x"])}
    arrays |= {f"in_{name}": np.ascontiguousarray(a) for name, a in laid.items()}
    nc = bacc.Bacc("TRN2", target_bir_lowering=False, num_devices=1)
    aps = {name.removeprefix("in_"): nc.dram_tensor(name, a.shape, my.dt.from_np(a.dtype), kind="ExternalInput").ap()
           for name, a in arrays.items()}
    out = nc.dram_tensor("out_x", (1, N, N, C), my.dt.float32, kind="ExternalOutput").ap()
    build_program(nc, aps.pop("x"), aps, out)
    return run_bass_kernel_spmd(nc, [arrays], core_ids=[0]).results[0]["out_x"]
```

```python
import concourse.bass as bass
from concourse import mybir
from contextlib import ExitStack

F32, BF16 = mybir.dt.float32, mybir.dt.bfloat16
ALU, ACT, AX = mybir.AluOpType, mybir.ActivationFunctionType, mybir.AxisListType

P = 128
N, C = 256, 128
L = N * N
PAD = N + 2
GN_EPS = LN_EPS = 1e-5
HEADS, HD = 4, 32


class Phase(ExitStack):

    def __init__(self, nc, kept):
        super().__init__()
        self.nc, self.kept, self.semaphores = nc, kept, []

    def semaphore(self, name):
        self.semaphores.append(self.enter_context(self.nc.semaphore(name)))
        return self.semaphores[-1]

    def kept_semaphore(self, name):
        return self.kept.enter_context(self.nc.semaphore(name))

    def clear_semaphores(self):
        with self.nc.Block() as block:

            @block.sync
            def _(sp):
                for semaphore in self.semaphores:
                    sp.sem_clear(semaphore)


def run_phase(nc, kept, phase, *args):
    with Phase(nc, kept) as es:
        phase(nc, es, *args)
    es.clear_semaphores()


class Tile:

    def __init__(self, i, j, J):
        self.i, self.j, self.J = i, j, J

    def upto(self, per=1, plus=0):
        return self.i * (self.J * per) + (self.j * per + plus)

    def loads(self, room=0):
        return self.i * 16 + 16

    def moved(self, d):
        j = self.j + d
        return Tile(self.i + j // self.J, j % self.J, self.J)

    def number(self):
        return self.i * self.J + self.j if isinstance(self.i, int) else None


def wait(eng, semaphore, value):
    if not isinstance(value, int) or value > 0:
        eng.wait_ge(semaphore, value)


def for_tiles(eng, tiles, J, body, alone=1):
    for i in range(alone):
        for j in range(J):
            body(Tile(i, j, J))
    with eng.Fori(alone, tiles // J - 1) as i:
        for j in range(J):
            body(Tile(i, j, J))
    for j in range(J):
        body(Tile(tiles // J - 1, j, J))


def is_last(tile, tiles):
    return tile.number() == tiles - 1


def build_identity(pool, nc, ident, done, at):
    nc.gpsimd.memset(ident[:, :], 0.0).then_inc(done, 1)
    pool.wait_ge(done, at + 1)
    nc.gpsimd.affine_select(out=ident[:, :], in_=ident[:, :], compare_op=ALU.not_equal, fill=1.0,
                            base=0, pattern=[[-1, P]], channel_multiplier=1).then_inc(done, 1)


def transpose_phase(nc, es, x, xT_dram, stats, tag="tr"):
    T, J = 512, 4
    tiles = L // T
    Q = T // P
    sb = lambda name, shape: es.enter_context(nc.sbuf_tensor(f"{tag}_{name}", shape, F32))
    sem = lambda name: es.semaphore(f"{tag}_{name}")
    ident, xin, xT = sb("ident", [P, P]), sb("xin", [P, J, Q, C]), sb("xT", [P, J, T])
    t_ps = es.enter_context(nc.psum_tensor(f"{tag}_ps", [P, J, Q, P], F32))
    ident_built, transposed, copied, measured = sem("ident_built"), sem("transposed"), sem("copied"), sem("measured")
    x_loaded = [sem(f"x_loaded{j}") for j in range(J)]
    xT_stored = [es.kept_semaphore(f"{tag}_xT_stored{j}") for j in range(J)]
    block = es.enter_context(nc.Block())

    @block.sync
    def _(sp):
        def body(t):
            wait(sp, transposed, t.upto(1, 1 - J))
            sp.dma_start(xin[:, t.j, :, :],
                         x[bass.ds(t.upto(T), T), :].rearrange("(p q) c -> p q c", q=Q)).then_inc(x_loaded[t.j], 16)

        for_tiles(sp, tiles, J, body)

    @block.gpsimd
    def _(pool):
        build_identity(pool, nc, ident, ident_built, 0)

        def body(t):
            wait(pool, copied, t.upto(1, 1))
            pool.dma_start(xT_dram[:, bass.ds(t.upto(T), T)], xT[:, t.j, :]).then_inc(xT_stored[t.j], 16)

        for_tiles(pool, tiles, J, body)
        for j in range(J):
            pool.wait_ge(xT_stored[j], tiles // J * 16)

    @block.tensor
    def _(pe):
        pe.wait_ge(ident_built, 2)

        def body(t):
            wait(pe, x_loaded[t.j], t.loads())
            wait(pe, copied, t.upto(1, 1 - J))
            for q in range(Q):
                ins = nc.tensor.transpose(t_ps[:, t.j, q, :], xin[:, t.j, q, :], ident[:, :])
            ins.then_inc(transposed, 1)

        for_tiles(pe, tiles, J, body)

    @block.scalar
    def _(act):
        def body(t):
            wait(act, transposed, t.upto(1, 1))
            wait(act, xT_stored[t.j], t.loads() - 16)
            wait(act, measured, t.upto(1, 1 - J))
            nc.scalar.activation(xT[:, t.j, :].rearrange("c (p q) -> c q p", q=Q), t_ps[:, t.j, :, :],
                                 ACT.Copy).then_inc(copied, 1)

        for_tiles(act, tiles, J, body)

    @block.vector
    def _(dve):
        def body(t):
            wait(dve, copied, t.upto(1, 1))
            nc.vector.bn_stats(stats[:, bass.ds(t.upto(1), 1), :].rearrange("p a b -> p (a b)"), xT[:, t.j, :])\
              .then_inc(measured, 1)

        for_tiles(dve, tiles, J, body)


def norm_phase(nc, es, stats, mean, rstd, tag):
    G = 4
    sb = lambda name, shape: es.enter_context(nc.sbuf_tensor(f"{tag}_{name}", shape, F32))
    sem = lambda name: es.semaphore(f"{tag}_{name}")
    average, mv, moments = sb("average", [P, P]), sb("mv", [P, 2]), sb("moments", [P, 2])
    square, var = sb("square", [P, 1]), sb("var", [P, 1])
    m_ps = es.enter_context(nc.psum_tensor(f"{tag}_ps", [P, 2], F32))
    averager_built, step, averaged = sem("averager_built"), sem("step"), sem("averaged")
    root_taken = sem("root_taken")
    block = es.enter_context(nc.Block())

    @block.gpsimd
    def _(pool):
        view = average[:, :].rearrange("p (g j) -> p g j", j=G)
        nc.gpsimd.memset(average[:, :], 1.0 / G).then_inc(averager_built, 1)
        pool.wait_ge(averager_built, 1)
        nc.gpsimd.affine_select(out=view, in_=view, compare_op=ALU.is_ge, fill=0.0, base=0,
                                pattern=[[-G, P // G], [0, G]], channel_multiplier=1).then_inc(averager_built, 1)
        pool.wait_ge(averager_built, 2)
        nc.gpsimd.affine_select(out=view, in_=view, compare_op=ALU.is_ge, fill=0.0, base=G - 1,
                                pattern=[[G, P // G], [0, G]], channel_multiplier=-1).then_inc(averager_built, 1)

    @block.tensor
    def _(pe):
        pe.wait_ge(averager_built, 3)
        pe.wait_ge(step, 4)
        nc.tensor.matmul(m_ps[:, :], average[:, :], moments[:, :], start=True, stop=True).then_inc(averaged, 1)

    @block.vector
    def _(dve):
        made = [0]

        def chained(ins):
            made[0] += 1
            ins.then_inc(step, 1)
            dve.wait_ge(step, made[0])

        chained(nc.vector.bn_aggr(mv[:, :], stats[:, :, :]))
        chained(nc.vector.tensor_tensor(square[:, :], mv[:, 0:1], mv[:, 0:1], ALU.mult))
        chained(nc.vector.tensor_copy(moments[:, 0:1], mv[:, 0:1]))
        chained(nc.vector.tensor_tensor(moments[:, 1:2], mv[:, 1:2], square[:, :], ALU.add))
        dve.wait_ge(averaged, 1)
        chained(nc.vector.tensor_copy(mean[:, :], m_ps[:, 0:1]))
        chained(nc.vector.tensor_tensor(square[:, :], mean[:, :], mean[:, :], ALU.mult))
        chained(nc.vector.tensor_tensor(var[:, :], m_ps[:, 1:2], square[:, :], ALU.subtract))
        chained(nc.vector.tensor_scalar(var[:, :], var[:, :], GN_EPS, None, ALU.add))
        dve.wait_ge(root_taken, 1)
        chained(nc.vector.reciprocal(rstd[:, :], var[:, :]))

    @block.scalar
    def _(act):
        act.wait_ge(step, 8)
        nc.scalar.activation(var[:, :], var[:, :], ACT.Sqrt).then_inc(root_taken, 1)


def bias_phase(nc, es, xT_dram, mean, rstd, w_bias, bias_dram):
    T, J = 512, 4
    tiles = L // T
    sb = lambda name, shape: es.enter_context(nc.sbuf_tensor(f"bi_{name}", shape, F32))
    sem = lambda name: es.semaphore(f"bi_{name}")
    wb, xT, xn, out = sb("wb", [P, HEADS]), sb("xT", [P, J, T]), sb("xn", [P, J, T]), sb("out", [HEADS, J, T])
    b_ps = es.enter_context(nc.psum_tensor("bi_ps", [HEADS, J, T], F32))
    w_loaded, normed, projected, copied = sem("w_loaded"), sem("normed"), sem("projected"), sem("copied")
    x_loaded = [sem(f"x_loaded{j}") for j in range(J)]
    stored = [es.kept_semaphore(f"bi_stored{j}") for j in range(J)]
    block = es.enter_context(nc.Block())

    @block.sync
    def _(sp):
        sp.dma_start(wb[:, :], w_bias).then_inc(w_loaded, 16)

        def body(t):
            wait(sp, normed, t.upto(1, 1 - J))
            sp.dma_start(xT[:, t.j, :], xT_dram[:, bass.ds(t.upto(T), T)]).then_inc(x_loaded[t.j], 16)

        for_tiles(sp, tiles, J, body)

    @block.vector
    def _(dve):
        def body(t):
            wait(dve, x_loaded[t.j], t.loads())
            wait(dve, projected, t.upto(1, 1 - J))
            nc.vector.tensor_scalar(xn[:, t.j, :], xT[:, t.j, :], mean[:, :], rstd[:, :], ALU.subtract, ALU.mult)\
              .then_inc(normed, 1)

        for_tiles(dve, tiles, J, body)

    @block.tensor
    def _(pe):
        pe.wait_ge(w_loaded, 16)

        def body(t):
            wait(pe, normed, t.upto(1, 1))
            wait(pe, copied, t.upto(1, 1 - J))
            nc.tensor.matmul(b_ps[:, t.j, :], wb[:, :], xn[:, t.j, :], start=True, stop=True).then_inc(projected, 1)

        for_tiles(pe, tiles, J, body)

    @block.scalar
    def _(act):
        def body(t):
            wait(act, projected, t.upto(1, 1))
            wait(act, stored[t.j], t.loads() - 16)
            nc.scalar.activation(out[:, t.j, :], b_ps[:, t.j, :], ACT.Copy).then_inc(copied, 1)

        for_tiles(act, tiles, J, body)

    @block.gpsimd
    def _(pool):
        def body(t):
            wait(pool, copied, t.upto(1, 1))
            pool.dma_start(bias_dram[:, bass.ds(t.upto(T), T)], out[:, t.j, :]).then_inc(stored[t.j], 16)

        for_tiles(pool, tiles, J, body)
        for j in range(J):
            pool.wait_ge(stored[j], tiles // J * 16)


def attention_phase(nc, es, w, xT_dram, bias_dram, mean, rstd, x1_dram, stats):
    T, J = 2 * N, 2
    tiles, BLOCKS = L // T, 4
    KC = N // P
    SCALE = float(C) ** -0.5

    sb = lambda name, shape: es.enter_context(nc.sbuf_tensor(f"at_{name}", shape, F32))
    ps = lambda name, shape: es.enter_context(nc.psum_tensor(f"at_{name}", shape, F32))
    sem = lambda name: es.semaphore(f"at_{name}")

    ident = sb("ident", [P, P])
    wqkvg, wo = sb("wqkvg", [P, 4, C]), sb("wo", [P, C])
    bias = sb("bias", [P, KC, HEADS, N])
    xT, xn, xres = sb("xT", [P, J, T]), sb("xn", [P, J, T]), sb("xres", [P, J, T])
    q = sb("q", [P, J, HEADS, T])
    k, v = sb("k", [P, J, T]), sb("v", [P, J, T // P, C])
    gate = sb("gate", [P, J, T])
    S, E = sb("S", [P, 2, HEADS, N]), sb("E", [P, 2, HEADS, N])
    top, low = sb("top", [P, 4, HEADS]), sb("low", [P, 4, HEADS])
    total, inverse = sb("total", [P, 4, HEADS]), sb("inverse", [P, 4, HEADS])
    ones, inverse_wide = sb("ones", [P, HEADS, HD]), sb("inverse_wide", [P, 2, C])
    ET = sb("ET", [P, 2, HEADS, KC, P])
    OT, OT_inverse = sb("OT", [P, J, T]), sb("OT_inverse", [P, P])
    gated = sb("gated", [P, T])
    x1 = sb("x1", [P, J, 2, PAD])
    margin = sb("margin", [P, PAD])

    S_ps, ET_ps = ps("S_ps", [P, HEADS, N]), ps("ET_ps", [P, HEADS, KC, P])
    pr_ps = ps("pr_ps", [P, 2, T])
    OT_ps, inverse_ps = ps("OT_ps", [P, T]), ps("inverse_ps", [P, T])

    ident_built, w_loaded, margin_stored, zeroed = (
        sem("ident_built"), sem("w_loaded"), sem("margin_stored"), sem("zeroed"))
    x_loaded, res_loaded, x1_stored = ([sem(f"{s}{j}") for j in range(J)]
                                       for s in ("x_loaded", "res_loaded", "x1_stored"))
    normed, q_made, k_made, g_made, v_made, out_made = map(
        sem, ("normed", "q_made", "k_made", "g_made", "v_made", "out_made"))
    q_copied, k_copied, g_exp, v_copied = map(sem, ("q_copied", "k_copied", "g_exp", "v_copied"))
    gate_step, gated_made, x1_made, measured = map(sem, ("gate_step", "gated_made", "x1_made", "measured"))
    scored, biased, topped, lowered, exped = map(sem, ("scored", "biased", "topped", "lowered", "exped"))
    inverse_spread = sem("inverse_spread")
    turned, ET_copied, inverted, inverse_turned, inverse_copied, weighed, OT_made = map(
        sem, ("turned", "ET_copied", "inverted", "inverse_turned", "inverse_copied", "weighed", "OT_made"))

    block = es.enter_context(nc.Block())

    def count(t, b):
        return t.upto(BLOCKS, b + 1)

    @block.sync
    def _(sp):
        for i, name in enumerate(("Wq", "Wk", "Wv", "Wg")):
            sp.dma_start(wqkvg[:, i, :], w[name]).then_inc(w_loaded, 16)
        sp.dma_start(wo[:, :], w["Wo"]).then_inc(w_loaded, 16)
        for qc in range(KC):
            sp.dma_start(bias[:, qc, :, :],
                         bias_dram.rearrange("h (c q k) -> q c h k", c=KC, k=N)[:, qc, :, :]).then_inc(w_loaded, 16)
        sp.wait_ge(zeroed, 4)
        for row in (0, PAD - 1):
            sp.dma_start(x1_dram[:, row, :], margin[:, :]).then_inc(margin_stored, 16)

        def load(t):
            wait(sp, normed, t.upto(1, 1 - J))
            sp.dma_start(xT[:, t.j, :], xT_dram[:, bass.ds(t.upto(T), T)]).then_inc(x_loaded[t.j], 16)

        def load_residual(t):
            sp.dma_start(xres[:, t.j, :], xT_dram[:, bass.ds(t.upto(T), T)]).then_inc(res_loaded[t.j], 16)

        def store(t):
            wait(sp, x1_made, t.upto(1, 1))
            sp.dma_start(x1_dram[:, bass.ds(t.upto(2, 1), 2), :], x1[:, t.j, :, :]).then_inc(x1_stored[t.j], 16)

        def body(t):
            if not is_last(t, tiles):
                load(t.moved(1))
            if t.number() not in (0, 1):
                store(t.moved(-J))
            load_residual(t)

        load(Tile(0, 0, J))
        for_tiles(sp, tiles, J, body, alone=2)
        for j in range(J):
            store(Tile(tiles // J - 1, j, J))
        for j in range(J):
            sp.wait_ge(x1_stored[j], tiles // J * 16)
        sp.wait_ge(margin_stored, 2 * 16)

    @block.gpsimd
    def _(pool):
        build_identity(pool, nc, ident, ident_built, 0)
        nc.gpsimd.memset(margin[:, :], 0.0).then_inc(zeroed, 1)
        nc.gpsimd.memset(x1[:, :, :, :], 0.0).then_inc(zeroed, 1)
        nc.gpsimd.memset(q[:, :, :, :], 0.0).then_inc(zeroed, 1)
        nc.gpsimd.memset(ones[:, :, :], 1.0).then_inc(zeroed, 1)

        def spread_inverse(t, b):
            wait(pool, inverted, count(t, b))
            wait(pool, inverse_turned, count(t, b - 2))
            nc.gpsimd.tensor_tensor(inverse_wide[:, b % 2, :].rearrange("p (h d) -> p h d", h=HEADS),
                                    inverse[:, b, :].unsqueeze(2).to_broadcast([P, HEADS, HD]), ones[:, :, :],
                                    ALU.mult).then_inc(inverse_spread, 1)

        def finish(t):
            wait(pool, gated_made, t.upto(1, 1))
            wait(pool, res_loaded[t.j], t.loads())
            wait(pool, x1_stored[t.j], t.loads() - 16)
            wait(pool, measured, t.upto(1, 1 - J))
            nc.gpsimd.tensor_tensor(x1[:, t.j, :, 1:N + 1], gated[:, :].rearrange("c (r p) -> c r p", r=2),
                                    xres[:, t.j, :].rearrange("c (r p) -> c r p", r=2), ALU.add).then_inc(x1_made, 1)

        def body(t):
            for b in range(BLOCKS):
                if b >= 1:
                    spread_inverse(t, b - 1)
                elif t.number() != 0:
                    spread_inverse(t.moved(-1), BLOCKS - 1)
                if b == 3 and t.number() != 0:
                    finish(t.moved(-1))

        pool.wait_ge(zeroed, 4)
        for_tiles(pool, tiles, J, body, alone=2)
        spread_inverse(Tile(tiles // J - 1, J - 1, J), BLOCKS - 1)
        finish(Tile(tiles // J - 1, J - 1, J))

    @block.tensor
    def _(pe):
        pe.wait_ge(ident_built, 2)
        pe.wait_ge(w_loaded, 7 * 16)

        def project(t, which):
            if which < 2:
                wait(pe, normed, t.upto(1, 1))
            if which == 0:
                wait(pe, g_exp, t.upto(1, 0))
                nc.tensor.matmul(pr_ps[:, 0, :], wqkvg[:, 0, :], xn[:, t.j, :], start=True, stop=True)\
                  .then_inc(q_made, 1)
            elif which == 1:
                wait(pe, v_copied, t.upto(1, 0))
                nc.tensor.matmul(pr_ps[:, 1, :], wqkvg[:, 1, :], xn[:, t.j, :], start=True, stop=True)\
                  .then_inc(k_made, 1)
            elif which == 2:
                wait(pe, q_copied, t.upto(1, 1))
                wait(pe, gated_made, t.upto(1, -1))
                nc.tensor.matmul(pr_ps[:, 0, :], wqkvg[:, 3, :], xn[:, t.j, :], start=True, stop=True)\
                  .then_inc(g_made, 1)
            else:
                wait(pe, k_copied, t.upto(1, 1))
                for c in range(T // P):
                    ins = nc.tensor.matmul(pr_ps[:, 1, c * P:(c + 1) * P], xn[:, t.j, c * P:(c + 1) * P],
                                           wqkvg[:, 2, :], start=True, stop=True)
                ins.then_inc(v_made, 1)

        def score(t, b):
            row, qc = b // KC, b % KC
            if b == 0:
                wait(pe, q_copied, t.upto(1, 1))
                wait(pe, k_copied, t.upto(1, 1))
            wait(pe, biased, count(t, b - 1))
            q0, k0 = row * N + qc * P, row * N
            for h in range(HEADS):
                ins = nc.tensor.matmul(S_ps[:, h, :], q[:, t.j, h, q0:q0 + P], k[:, t.j, k0:k0 + N],
                                       start=True, stop=True)
            ins.then_inc(scored, 1)

        def turn(t, b):
            wait(pe, exped, count(t, b))
            wait(pe, ET_copied, count(t, b - 1))
            for h in range(HEADS):
                for kc in range(KC):
                    ins = nc.tensor.transpose(ET_ps[:, h, kc, :], E[:, b % 2, h, kc * P:(kc + 1) * P], ident[:, :])
            ins.then_inc(turned, 1)

        def turn_inverse(t, b):
            wait(pe, inverse_spread, count(t, b))
            wait(pe, OT_made, count(t, b - 1))
            nc.tensor.transpose(inverse_ps[:, 0:P], inverse_wide[:, b % 2, :], ident[:, :]).then_inc(inverse_turned, 1)

        def weigh(t, b):
            if b == 0:
                wait(pe, v_copied, t.upto(1, 1))
            wait(pe, ET_copied, count(t, b))
            wait(pe, OT_made, count(t, b - 1))
            for h in range(HEADS):
                channels = slice(h * HD, (h + 1) * HD)
                for kc in range(KC):
                    ins = nc.tensor.matmul(OT_ps[channels, 0:P], v[:, t.j, b // KC * KC + kc, channels],
                                           ET[:, b % 2, h, kc, :], start=kc == 0, stop=kc == KC - 1,
                                           tile_position=(0, h * HD))
            ins.then_inc(weighed, 1)

        def output(t, ahead):
            wait(pe, OT_made, count(t, BLOCKS - 1))
            wait(pe, q_copied, t.upto(1, 1 + ahead))
            wait(pe, g_exp, t.upto(1, 1 + min(ahead, 1)))
            wait(pe, gated_made, t.upto(1, 0))
            nc.tensor.matmul(pr_ps[:, 0, :], wo[:, :], OT[:, t.j, :], start=True, stop=True).then_inc(out_made, 1)

        def body(t):
            after = None if is_last(t, tiles) else t.moved(1)
            before = None if t.number() == 0 else t.moved(-1)
            for b in range(BLOCKS):
                if b < BLOCKS - 1:
                    score(t, b + 1)
                elif after:
                    score(after, 0)
                behind = (t, b - 2) if b >= 2 else (before, b + BLOCKS - 2) if before else None
                if behind:
                    turn_inverse(*behind)
                    weigh(*behind)
                if b == 1 and after:
                    project(after, 1)
                if b == 3 and after:
                    project(after, 3)
                turn(t, b)
                if b == 0:
                    project(t, 2)
                if b == 1 and after:
                    project(after, 0)
                if b == 3 and before:
                    output(before, 2 if after else 1)

        first, last = Tile(0, 0, J), Tile(tiles // J - 1, J - 1, J)
        for which in (0, 1, 3):
            project(first, which)
        score(first, 0)
        for_tiles(pe, tiles, J, body, alone=2)
        for b in (BLOCKS - 2, BLOCKS - 1):
            turn_inverse(last, b)
            weigh(last, b)
        output(last, 0)

    @block.scalar
    def _(act):
        act.preload_act_table_set("natural_log_exp_and_others")

        def copy_q(t):
            wait(act, q_made, t.upto(1, 1))
            wait(act, scored, count(t, 3 - 4 * J))
            for h in range(HEADS):
                rows = slice(h * HD, (h + 1) * HD)
                ins = nc.scalar.activation(q[rows, t.j, h, :], pr_ps[rows, 0, :], ACT.Copy, scale=SCALE)
            ins.then_inc(q_copied, 1)

        def exp_g(t):
            wait(act, g_made, t.upto(1, 1))
            wait(act, gated_made, t.upto(1, 1 - J))
            nc.scalar.activation(gate[:, t.j, :], pr_ps[:, 0, :], ACT.Exp, scale=-1.0).then_inc(g_exp, 1)

        def exps(t, b):
            wait(act, lowered, count(t, b))
            wait(act, turned, count(t, b - 2))
            wait(act, inverted, count(t, b - 4))
            for h in range(HEADS):
                ins = nc.scalar.activation(E[:, b % 2, h, :], S[:, b % 2, h, :], ACT.Exp, bias=low[:, b, h:h + 1],
                                           accum_out=total[:, b, h:h + 1])
            ins.then_inc(exped, 1)

        def copy_ET(t, b):
            wait(act, turned, count(t, b))
            wait(act, weighed, count(t, b - 2))
            nc.scalar.activation(ET[:, b % 2, :, :, :], ET_ps[:, :, :, :], ACT.Copy).then_inc(ET_copied, 1)

        def body(t):
            after = None if is_last(t, tiles) else t.moved(1)
            before = None if t.number() == 0 else t.moved(-1)
            for b in range(BLOCKS):
                if b >= 1:
                    copy_ET(t, b - 1)
                elif before:
                    copy_ET(before, BLOCKS - 1)
                exps(t, b)
                if after and b == 2:
                    copy_q(after)
                if b == 0:
                    exp_g(t)

        first, last = Tile(0, 0, J), Tile(tiles // J - 1, J - 1, J)
        act.wait_ge(zeroed, 4)
        copy_q(first)
        for_tiles(act, tiles, J, body, alone=2)
        copy_ET(last, BLOCKS - 1)

    @block.vector
    def _(dve):
        def norm(t):
            wait(dve, x_loaded[t.j], t.loads())
            wait(dve, v_made, t.upto(1, 1 - J))
            wait(dve, g_made, t.upto(1, 1 - J))
            nc.vector.tensor_scalar(xn[:, t.j, :], xT[:, t.j, :], mean[:, :], rstd[:, :], ALU.subtract, ALU.mult)\
              .then_inc(normed, 1)

        def copy_k(t):
            wait(dve, k_made, t.upto(1, 1))
            wait(dve, scored, count(t, 3 - 4 * J))
            nc.vector.tensor_copy(k[:, t.j, :], pr_ps[:, 1, :]).then_inc(k_copied, 1)

        def copy_v(t):
            wait(dve, v_made, t.upto(1, 1))
            wait(dve, weighed, count(t, 3 - 4 * J))
            nc.vector.tensor_copy(v[:, t.j, :, :], pr_ps[:, 1, :].rearrange("p (c d) -> p c d", d=C))\
              .then_inc(v_copied, 1)

        def make_gate(t, stage):
            if stage == 0:
                wait(dve, g_exp, t.upto(1, 1))
                nc.vector.tensor_scalar(gate[:, t.j, :], gate[:, t.j, :], 1.0, None, ALU.add).then_inc(gate_step, 1)
            else:
                part = slice((stage - 1) * P, stage * P)
                wait(dve, gate_step, t.upto(1 + T // P, 1))
                nc.vector.reciprocal(gate[:, t.j, part], gate[:, t.j, part]).then_inc(gate_step, 1)

        def maximum(t, b):
            wait(dve, scored, count(t, b))
            wait(dve, exped, count(t, b - 2))
            wait(dve, lowered, count(t, b - 4))
            nc.vector.tensor_tensor(S[:, b % 2, :, :], S_ps[:, :, :], bias[:, b % KC, :, :], ALU.add)\
              .then_inc(biased, 1)
            wait(dve, biased, count(t, b))
            nc.vector.tensor_reduce(top[:, b, :], S[:, b % 2, :, :], AX.X, ALU.max).then_inc(topped, 1)

        def negate(t, b):
            wait(dve, topped, count(t, b))
            nc.vector.tensor_scalar(low[:, b, :], top[:, b, :], -1.0, None, ALU.mult).then_inc(lowered, 1)

        def invert(t, b):
            wait(dve, exped, count(t, b))
            wait(dve, inverse_spread, count(t, b - 4))
            nc.vector.reciprocal(inverse[:, b, :], total[:, b, :]).then_inc(inverted, 1)

        def make_OT(t, b):
            wait(dve, weighed, count(t, b))
            wait(dve, inverse_turned, count(t, b))
            wait(dve, out_made, t.upto(1, 1 - J))
            wait(dve, OT_made, count(t, b - 1))
            nc.vector.tensor_copy(OT_inverse[:, :], inverse_ps[:, 0:P]).then_inc(inverse_copied, 1)
            wait(dve, inverse_copied, count(t, b))
            nc.vector.tensor_tensor(OT[:, t.j, b * P:(b + 1) * P], OT_ps[:, 0:P], OT_inverse[:, :], ALU.mult)              .then_inc(OT_made, 1)

        def make_gated(t):
            wait(dve, out_made, t.upto(1, 1))
            wait(dve, gate_step, t.upto(1 + T // P, 1 + T // P))
            wait(dve, x1_made, t.upto(1, 0))
            nc.vector.tensor_tensor(gated[:, :], pr_ps[:, 0, :], gate[:, t.j, :], ALU.mult).then_inc(gated_made, 1)

        def measure(t):
            wait(dve, x1_made, t.upto(1, 1))
            nc.vector.bn_stats(stats[:, bass.ds(t.upto(1), 1), :].rearrange("p a b -> p (a b)"),
                               x1[:, t.j, :, 1:N + 1]).then_inc(measured, 1)

        def body(t):
            after = None if is_last(t, tiles) else t.moved(1)
            before = None if t.number() == 0 else t.moved(-1)
            for b in range(BLOCKS):
                if b == 0:
                    copy_v(t)
                if b < BLOCKS - 1:
                    maximum(t, b + 1)
                    negate(t, b + 1)
                elif after:
                    maximum(after, 0)
                    negate(after, 0)
                if b >= 1:
                    invert(t, b - 1)
                elif before:
                    invert(before, BLOCKS - 1)
                if b >= 2:
                    make_OT(t, b - 2)
                elif before:
                    make_OT(before, b + BLOCKS - 2)
                if after and b == 0:
                    norm(after)
                if after and b == 1:
                    copy_k(after)
                if b < 3 and before:
                    make_gate(before, b + 2)
                if b == 2:
                    make_gate(t, 0)
                if b == 0 and before and t.number() != 1:
                    measure(t.moved(-2))
                if b == 3:
                    if before:
                        make_gated(before)
                    make_gate(t, 1)

        first, last = Tile(0, 0, J), Tile(tiles // J - 1, J - 1, J)
        norm(first)
        copy_k(first)
        maximum(first, 0)
        negate(first, 0)
        for_tiles(dve, tiles, J, body, alone=2)
        invert(last, BLOCKS - 1)
        for b in (BLOCKS - 2, BLOCKS - 1):
            make_OT(last, b)
        for stage in range(2, 5):
            make_gate(last, stage)
        measure(last.moved(-1))
        make_gated(last)
        measure(last)


WIN = 64
SIDE = N // WIN


class Window:

    def __init__(self, wy, v, j):
        self.wy, self.v, self.j = wy, v, j

    def upto(self, per=1, plus=0):
        return self.wy * (2 * per) + ((self.v * 2 * SIDE + self.j) * per + plus)

    def turns(self, per=1, plus=0):
        return self.wy * per + (self.v * SIDE * per + plus)

    def wx(self, per):
        return (self.v * 2 + self.j) * per

    def next(self):
        if self.j == 0:
            return Window(self.wy, self.v, 1)
        if isinstance(self.wy, int) and self.wy == SIDE - 1:
            return Window(0, self.v + 1, 0) if self.v + 1 < SIDE // 2 else None
        return Window(self.wy + 1, self.v, 0)


def for_window_pairs(eng, body, last_alone=False):
    body(0, 0)
    for v in range(SIDE // 2):
        with eng.Fori(1 if v == 0 else 0, SIDE - last_alone) as wy:
            body(wy, v)
        if last_alone:
            body(SIDE - 1, v)


def for_windows(eng, body):
    def pair(wy, v):
        for j in range(2):
            body(Window(wy, v, j))

    for_window_pairs(eng, pair, last_alone=True)


def conv_phase(nc, es, w, x1_dram, mean, rstd, u_dram):
    TAPS, FUSED, HALVES, ROWS = 9, 3, 2, 16
    SUMS = WIN // ROWS
    PAIRS, STEPS = SUMS // 2, TAPS - FUSED
    ADDED = SUMS * STEPS
    SIDE_IN = WIN + 2
    XCHUNKS = 9
    XCHUNK = SIDE_IN * SIDE_IN // XCHUNKS
    XBANKS = 4
    sb = lambda name, shape: es.enter_context(nc.sbuf_tensor(f"cv_{name}", shape, F32))
    sem = lambda name: es.semaphore(f"cv_{name}")
    win, taps = sb("win", [P, 2 * P]), sb("taps", [P, FUSED, 2 * P])
    wt = sb("wt", [P, FUSED, 2 * P])
    tap_w = sb("tap_w", [P, TAPS, HALVES])
    cb = sb("cb", [P, HALVES])
    inside = sb("inside", [P, SIDE * SIDE, 4])
    patch = sb("patch", [P, 2, SIDE_IN, SIDE_IN])
    raw = sb("raw", [P, SIDE_IN, SIDE_IN])
    xin = sb("xin", [P, HALVES, SIDE_IN, SIDE_IN])
    us = sb("us", [P, HALVES, WIN, WIN])
    uc = sb("uc", [P, HALVES, WIN, WIN])
    x_ps = es.enter_context(nc.psum_tensor("cv_x_ps", [P, XBANKS, 512], F32))
    c_ps = es.enter_context(nc.psum_tensor("cv_c_ps", [P, 2, ROWS * WIN], F32))
    w_loaded, w_made, masks_made, raw_loaded = map(sem, ("w_loaded", "w_made", "masks_made", "raw_loaded"))
    normed, edge, projected, xin_copied = map(sem, ("normed", "edge", "projected", "xin_copied"))
    summed, added, activated = map(sem, ("summed", "added", "activated"))
    turned = [sem(f"turned{h}") for h in range(HALVES)]
    us_stored, uc_stored = ([es.kept_semaphore(f"cv_{s}_stored{h}") for h in range(HALVES)] for s in ("us", "uc"))
    block = es.enter_context(nc.Block())

    def xchunks(t, half, c):
        return t.upto(HALVES * XCHUNKS, half * XCHUNKS + c)

    def adds(t, half, pair=0, step=0, m=0):
        return t.upto(HALVES * ADDED, half * ADDED + (pair * STEPS + step) * 2 + m)

    def next_half(t, half):
        return (t, 1) if half == 0 else (t.next(), 0) if t.next() else None

    @block.sync
    def _(sp):
        sp.dma_start(win[:, :], w["W_in"][:, 0:2 * P]).then_inc(w_loaded, 16)
        sp.dma_start(taps[:, :, :].rearrange("p t d -> p (t d)"),
                     w["conv_w"][0:FUSED * 2 * P].partition_broadcast(P)).then_inc(w_loaded, 16)
        with nc.allow_non_contiguous_dma("the taps' weights by channel, once"):
            for half in range(HALVES):
                sp.dma_start(tap_w[:, :, half], w["conv_w"].rearrange("(t s p) -> s p t", s=HALVES, p=P)[half])\
                  .then_inc(w_loaded, 16)
        sp.dma_start(cb[:, :], w["conv_b"]).then_inc(w_loaded, 16)

        def load(t):
            wait(sp, normed, t.upto())
            sp.dma_start(raw[:, :, :], x1_dram[:, bass.ds(t.wy * WIN, SIDE_IN), bass.ds(t.wx(WIN), SIDE_IN)])\
              .then_inc(raw_loaded, 16)

        for_windows(sp, load)

    @block.gpsimd
    def _(pool):
        def store(t):
            rows_at = t.wy * (SIDE * WIN * WIN) + t.wx(WIN * WIN)
            columns_at = t.wx(SIDE * WIN * WIN) + t.wy * (WIN * WIN)
            for half in range(HALVES):
                wait(pool, activated, t.upto(HALVES, half + 1))
                pool.dma_start(u_dram[0, half][:, bass.ds(rows_at, WIN * WIN)],
                               us[:, half, :, :].rearrange("p a b -> p (a b)")).then_inc(us_stored[half], 16)
                wait(pool, turned[half], t.upto(1, 1))
                pool.dma_start(u_dram[1, half][:, bass.ds(columns_at, WIN * WIN)],
                               uc[:, half, :, :].rearrange("p a b -> p (a b)")).then_inc(uc_stored[half], 16)

        for_windows(pool, store)
        for half in range(HALVES):
            pool.wait_ge(us_stored[half], SIDE * SIDE * 16)
            pool.wait_ge(uc_stored[half], SIDE * SIDE * 16)

    @block.vector
    def _(dve):
        nc.vector.memset(inside[:, :, :], 1.0).then_inc(masks_made, 1)
        edges = inside[:, :, :].rearrange("p (y x) e -> p y x e", x=SIDE)
        views = (edges[:, :, 0, 0], edges[:, :, SIDE - 1, 1], edges[:, 0, :, 2], edges[:, SIDE - 1, :, 3])
        dve.wait_ge(masks_made, 1)
        for view in views:
            nc.vector.memset(view, 0.0).then_inc(masks_made, 1)
        dve.wait_ge(w_loaded, 5 * 16)
        for tap in range(FUSED):
            ins = nc.vector.tensor_tensor(wt[:, tap, :], win[:, :], taps[:, tap, :], ALU.mult)
        ins.then_inc(w_made, 1)
        dve.wait_ge(masks_made, 5)

        def norm(t):
            wait(dve, raw_loaded, t.upto(16, 16))
            wait(dve, summed, t.upto(HALVES * SUMS, -HALVES * SUMS))
            nc.vector.tensor_scalar(patch[:, t.j, :, :], raw[:, :, :], mean[:, :], rstd[:, :], ALU.subtract, ALU.mult)\
              .then_inc(normed, 1)
            wait(dve, normed, t.upto(1, 1))
            for e, view in enumerate((patch[:, t.j, :, 0:1], patch[:, t.j, :, WIN + 1:], patch[:, t.j, 0:1, :],
                                      patch[:, t.j, WIN + 1:, :])):
                wait(dve, edge, t.upto(4, e))
                nc.vector.tensor_scalar(view, view, inside[:, bass.ds(t.wy * SIDE + t.wx(1), 1), e], None, ALU.mult)\
                  .then_inc(edge, 1)

        def add_tap(t, half, pair, step, m):
            tap, q = FUSED + step, pair * 2 + m
            dy, dx = tap // 3, tap % 3
            rows = us[:, half, q * ROWS:(q + 1) * ROWS, :]
            if step == 0:
                wait(dve, summed, t.upto(HALVES * SUMS, half * SUMS + q + 1))
                so_far = c_ps[:, m, :].rearrange("p (y x) -> p y x", x=WIN)
            else:
                wait(dve, added, adds(t, half, pair, step - 1, m) + 1)
                so_far = rows
            nc.vector.scalar_tensor_tensor(out=rows, in0=xin[:, half, q * ROWS + dy:(q + 1) * ROWS + dy, dx:dx + WIN],
                                           scalar=tap_w[:, tap, half:half + 1], in1=so_far,
                                           op0=ALU.mult, op1=ALU.add).then_inc(added, 1)

        def body(t):
            for half in range(HALVES):
                if half == 1 and t.next():
                    norm(t.next())
                wait(dve, xin_copied, xchunks(t, half, XCHUNKS))
                wait(dve, us_stored[half], t.upto(16))
                wait(dve, turned[half], t.upto())
                for pair in range(PAIRS):
                    for step in range(STEPS):
                        for m in range(2):
                            add_tap(t, half, pair, step, m)

        norm(Window(0, 0, 0))
        for_windows(dve, body)

    @block.tensor
    def _(pe):
        pe.wait_ge(w_made, 1)

        def project(t, half, chunks):
            for c in chunks:
                if half == 0 and c == 0:
                    wait(pe, edge, t.upto(4, 4))
                wait(pe, xin_copied, xchunks(t, half, c + 1 - XBANKS))
                nc.tensor.matmul(x_ps[:, ((t.j * HALVES + half) * XCHUNKS + c) % XBANKS, 0:XCHUNK],
                                 win[:, half * P:(half + 1) * P],
                                 patch[:, t.j, :, :].rearrange("p a b -> p (a b)")[:, c * XCHUNK:(c + 1) * XCHUNK],
                                 start=True, stop=True).then_inc(projected, 1)

        def add_fused(t, half, pair):
            for m in range(2):
                wait(pe, added, adds(t, half, pair - 1, 0, m) + 1)
                for part in range(2):
                    row = (pair * 2 + m) * ROWS + part * (ROWS // 2)
                    for tap in range(FUSED):
                        dy, dx = tap // 3, tap % 3
                        ins = nc.tensor.matmul(c_ps[:, m, part * 512:(part + 1) * 512], wt[:, tap, half * P:(half + 1) * P],
                                               patch[:, t.j, row + dy:row + dy + ROWS // 2, dx:dx + WIN],
                                               start=tap == 0, stop=tap == FUSED - 1)
                ins.then_inc(summed, 1)

        def body(t):
            for half in range(HALVES):
                after = next_half(t, half)
                for pair in range(PAIRS):
                    add_fused(t, half, pair)
                    if after:
                        project(*after, range(0, 5) if pair == 0 else range(5, XCHUNKS))

        project(Window(0, 0, 0), 0, range(XCHUNKS))
        for_windows(pe, body)

    @block.scalar
    def _(act):
        act.preload_act_table(ACT.Silu)
        act.wait_ge(w_loaded, 5 * 16)

        def copy_xin(t, half):
            wait(act, added, adds(t, half) - (HALVES - 1) * ADDED)
            for c in range(XCHUNKS):
                wait(act, projected, xchunks(t, half, c + 1))
                nc.scalar.activation(xin[:, half, :, :].rearrange("p a b -> p (a b)")[:, c * XCHUNK:(c + 1) * XCHUNK],
                                     x_ps[:, ((t.j * HALVES + half) * XCHUNKS + c) % XBANKS, 0:XCHUNK], ACT.Copy)\
                  .then_inc(xin_copied, 1)

        def activate(t, half):
            wait(act, added, adds(t, half) + ADDED)
            rows = us[:, half, :, :].rearrange("p a b -> p (a b)")
            nc.scalar.activation(rows, rows, ACT.Silu, bias=cb[:, half:half + 1]).then_inc(activated, 1)

        def turn(t, half):
            wait(act, activated, t.upto(HALVES, half + 1))
            wait(act, uc_stored[half], t.upto(16))
            nc.scalar.activation(uc[:, half, :, :], us[:, half, :, :].rearrange("p a b -> p b a"), ACT.Copy)\
              .then_inc(turned[half], 1)

        def body(t):
            for half in range(HALVES):
                if next_half(t, half):
                    copy_xin(*next_half(t, half))
                activate(t, half)
                turn(t, half)

        copy_xin(Window(0, 0, 0), 0)
        for_windows(act, body)


def scan_phase(nc, es, w, u_dram, y_dram, L):
    NS, R, DIRS, T = 16, 8, 4, 512
    NT = L // T
    NB, NU = 4, 4
    LAG = 3
    DT0 = 32
    PARTS = (0, 64, 96)

    def sb(name, shape, dt=F32):
        return es.enter_context(nc.sbuf_tensor("sc_" + name, shape, dt))

    def ps(name, shape):
        return es.enter_context(nc.psum_tensor("sc_" + name, shape, F32))

    def sem(name):
        return es.semaphore("sc_" + name)

    u = sb("u", [P, 2, 2, T])
    dt = sb("dt", [P, 2, 2, T])
    du = sb("du", [P, 2, 2, T])
    pre = sb("pre", [P, 2, T])
    spl = sb("spl", [P, 2, T])
    bc = sb("bc", [P, 2, T], BF16)
    rest = sb("rest", [P, T])
    dts = sb("dts", [DT0 + R, T])
    ROW, SEAM, SPAN = 2 * (T + 1), T, 2 * T + 1
    h = sb("h", [P, NS, ROW])
    dA = sb("dA", [P, NB, ROW])
    dBu = sb("dBu", [P, NU, ROW])
    yp = sb("yp", [P, 2, 2, T])
    Cb = sb("Cb", [P, NB, T])
    hC = sb("hC", [P, NB, 2, T])
    yo = sb("yo", [P, 2, 2, T])
    sel = sb("sel", [P, 2 * NS, P], BF16)
    ident = sb("ident", [P, P])
    xp = sb("xp", [P, DIRS, 2, P])
    dtw = sb("dtw", [DT0 + R, DIRS, 2, P])
    dtb = sb("dtb", [P, DIRS, 2])
    Dk = sb("Dk", [P, DIRS, 2])
    A = sb("A", [P, DIRS, 2, NS])
    xd_ps, dt_ps = ps("xd_ps", [P, T]), ps("dt_ps", [P, T])
    B_ps, C_ps, y_ps = ps("B_ps", [P, 2, T]), ps("C_ps", [P, 2, T]), ps("y_ps", [P, 2, T])

    weights_zeroed, weights_loaded = sem("weights_zeroed"), sem("weights_loaded")
    selectors_built, A_built = sem("selectors_built"), sem("A_built")
    u_loaded = [sem(f"u_loaded{j}") for j in range(2)]
    yp_loaded = [sem(f"yp_loaded{j}") for j in range(2)]
    y_stored = [sem(f"y_stored{j}") for j in range(2)]
    xd_made, dtraw_made = sem("xd_made"), sem("dtraw_made")
    high_made, mid_made, low_made = sem("high_made"), sem("mid_made"), sem("low_made")
    rest1_made, rest2_made = sem("rest1_made"), sem("rest2_made")
    pre_made, softplus_step = sem("pre_made"), sem("softplus_step")
    dt_made, du_made = sem("dt_made"), sem("du_made")
    B_made, C_made, y_summed = sem("B_made"), sem("C_made"), sem("y_summed")
    dA_made, Cb_made = sem("dA_made"), sem("Cb_made")
    seam_zeroed, h_zeroed, dBu_made, scanned = sem("seam_zeroed"), sem("h_zeroed"), sem("dBu_made"), sem("scanned")
    hC_made, skip_made, yo_made = sem("hC_made"), sem("skip_made"), sem("yo_made")

    def wait(eng, semaphore, value):
        if not isinstance(value, int) or value > 0:
            eng.wait_ge(semaphore, value)

    class Tile:

        def __init__(self, k, i, j):
            self.k, self.i, self.j = k, i, j

        def tiles(self, per=1, plus=0):
            return self.i * (2 * per) + ((self.k * NT + self.j) * per + plus)

        def loads(self):
            return self.i * 16 + (self.k * NT // 2 + 1) * 16

        def at(self):
            if self.k >= 2:
                return self.i * (-2 * T) + (NT - 1 - self.j) * T
            return self.i * (2 * T) + self.j * T

        def next(self):
            if self.j == 0:
                return Tile(self.k, self.i, 1)
            if isinstance(self.i, int) and self.i == NT // 2 - 1:
                return Tile(self.k + 1, 0, 0) if self.k + 1 < DIRS else None
            return Tile(self.k, self.i + 1, 0)

        def before(self):
            if self.j == 1:
                return Tile(self.k, self.i, 0)
            if isinstance(self.i, int) and self.i == 0:
                return Tile(self.k - 1, NT // 2 - 1, 1) if self.k else None
            return Tile(self.k, self.i - 1, 1)

        def order(self):
            return self.k % 2

        def first(self):
            return isinstance(self.i, int) and self.i == 0 and self.j == 0

    def for_tiles(eng, body):
        for k in range(DIRS):
            alone = 2 if k == 0 else 1
            for i in range(alone):
                body(Tile(k, i, 0))
                body(Tile(k, i, 1))
            with eng.Fori(alone, NT // 2 - 1) as i:
                body(Tile(k, i, 0))
                body(Tile(k, i, 1))
            body(Tile(k, NT // 2 - 1, 0))
            body(Tile(k, NT // 2 - 1, 1))

    def run(row, tile):
        return row[:, 0:SPAN][:, ::-1] if tile.k >= 2 else row[:, 0:SPAN]

    def halves(row):
        return row.rearrange("p (s t) -> p s t", s=2)[:, :, 0:T]

    def last_states(tile):
        return (T + 1, 0) if tile.k >= 2 else (T - 1, 2 * T)

    def both(ap):
        return ap.unsqueeze(1).to_broadcast([P, 2, T])

    block = es.enter_context(nc.Block())
    WEIGHT_DMAS = (len(PARTS) + 1) * 2 * DIRS + 4

    @block.sync
    def _(sp):
        sp.wait_ge(weights_zeroed, 1)
        for k in range(DIRS):
            for half in range(2):
                rows = w["x_proj"][k, half * P:(half + 1) * P, :]
                for part in PARTS:
                    sp.dma_start(xp[:, k, half, part:part + 2 * NS], rows[:, R:]).then_inc(weights_loaded, 16)
                sp.dma_start(xp[:, k, half, DT0:DT0 + R], rows[:, 0:R]).then_inc(weights_loaded, 16)
        sp.dma_start(dtw[DT0:DT0 + R, :, :, :], w["dt_w"]).then_inc(weights_loaded, 16)
        for here, there in ((dtb, w["dt_b"]), (Dk, w["D"]), (A, w["A_log"])):
            sp.dma_start(here[:], there).then_inc(weights_loaded, 16)

        def load_u(tile):
            sp.dma_start(u[:, tile.j, :, :],
                         u_dram[tile.order()].rearrange("s p l -> p s l")[:, :, bass.ds(tile.at(), T)])\
              .then_inc(u_loaded[tile.j], 16)

        def load_yp(tile):
            if tile.k < 2:
                return
            if tile.first():
                for j in range(2):
                    sp.wait_ge(y_stored[j], (tile.k - 1) * NT // 2 * 16)
            sp.dma_start(yp[:, tile.j, :, :],
                         y_dram[tile.k - 2].rearrange("s p l -> p s l")[:, :, bass.ds(tile.at(), T)])\
              .then_inc(yp_loaded[tile.j], 16)

        def store_y(tile):
            sp.dma_start(y_dram[tile.k].rearrange("s p l -> p s l")[:, :, bass.ds(tile.at(), T)],
                         yo[:, tile.j, :, :]).then_inc(y_stored[tile.j], 16)

        def body(tile):
            wait(sp, yo_made, tile.tiles())
            if tile.before():
                store_y(tile.before())
            if tile.next():
                load_yp(tile.next())
            if tile.next() and tile.next().next():
                wait(sp, du_made, tile.tiles(1, 1))
                wait(sp, skip_made, tile.tiles(1, 1))
                load_u(tile.next().next())

        load_u(Tile(0, 0, 0))
        load_u(Tile(0, 0, 1))
        for_tiles(sp, body)
        last = Tile(DIRS - 1, NT // 2 - 1, 1)
        sp.wait_ge(yo_made, DIRS * NT)
        store_y(last)
        for j in range(2):
            sp.wait_ge(y_stored[j], DIRS * NT // 2 * 16)

    @block.gpsimd
    def _(pool):
        nc.gpsimd.memset(xp[:, :, :, :], 0.0).then_inc(weights_zeroed, 1)
        nc.gpsimd.memset(ident[:, :], 0.0).then_inc(selectors_built, 1)
        nc.gpsimd.memset(sel[:, :, :], 0.0).then_inc(selectors_built, 1)
        pool.wait_ge(selectors_built, 2)
        nc.gpsimd.affine_select(out=ident[:, :], in_=ident[:, :], compare_op=ALU.not_equal, fill=1.0,
                                base=0, pattern=[[-1, P]], channel_multiplier=1).then_inc(selectors_built, 1)
        for n, part in enumerate(PARTS):
            pool.wait_ge(selectors_built, 3 + n)
            nc.gpsimd.affine_select(out=sel[:, :, :], in_=sel[:, :, :], compare_op=ALU.not_equal, fill=1.0,
                                    base=-part, pattern=[[-1, 2 * NS], [0, P]], channel_multiplier=1)\
              .then_inc(selectors_built, 1)

        def make_du(tile):
            wait(pool, dt_made, tile.tiles(1, 1))
            wait(pool, dBu_made, tile.tiles(NS, -NS))
            wait(pool, u_loaded[tile.j], tile.loads())
            nc.gpsimd.tensor_tensor(du[:, tile.j, :, :], dt[:, tile.j, :, :], u[:, tile.j, :, :], ALU.mult)\
              .then_inc(du_made, 1)

        def body(tile):
            for n in range(NS):
                wait(pool, scanned, tile.tiles(NS, n + 1))
                wait(pool, Cb_made, tile.tiles(NS, n + 1))
                wait(pool, y_summed, tile.tiles(NS, n + 1 - NB))
                nc.gpsimd.tensor_tensor(hC[:, n % NB, :, :], halves(h[:, n, :]), both(Cb[:, n % NB, :]), ALU.mult)\
                  .then_inc(hC_made, 1)
                if n == 10 and tile.next():
                    make_du(tile.next())

        make_du(Tile(0, 0, 0))
        for_tiles(pool, body)

    @block.scalar
    def _(act):
        act.preload_act_table_set("natural_log_exp_and_others")
        act.wait_ge(weights_loaded, WEIGHT_DMAS * 16)
        nc.scalar.activation(A[:, :, :, :], A[:, :, :, :], ACT.Exp).then_inc(A_built, 1)
        act.wait_ge(A_built, 1)
        nc.scalar.mul(A[:, :, :, :], A[:, :, :, :], -1.0).then_inc(A_built, 1)
        act.wait_ge(A_built, 2)

        def high(tile):
            wait(act, xd_made, tile.tiles(1, 1))
            wait(act, C_made, tile.tiles(NS, -NS))
            wait(act, low_made, tile.tiles(1, 0))
            wait(act, dtraw_made, tile.tiles(2, 0))
            nc.scalar.activation(bc[:, tile.j, :], xd_ps[:, :], ACT.Copy)
            nc.scalar.activation(dts[DT0:DT0 + R, :], xd_ps[DT0:DT0 + R, :], ACT.Copy).then_inc(high_made, 1)

        def middle(tile):
            wait(act, rest1_made, tile.tiles(1, 1))
            nc.scalar.activation(bc[64:P, tile.j, :], rest[64:P, :], ACT.Copy).then_inc(mid_made, 1)

        def low(tile):
            wait(act, rest2_made, tile.tiles(1, 1))
            nc.scalar.activation(bc[96:P, tile.j, :], rest[96:P, :], ACT.Copy).then_inc(low_made, 1)

        def add_bias(tile, half):
            wait(act, dtraw_made, tile.tiles(2, half + 1))
            wait(act, dt_made, tile.tiles(1, 0))
            nc.scalar.activation(pre[:, half, :], dt_ps[:, :], ACT.Identity,
                                 bias=dtb[:, tile.k, half:half + 1]).then_inc(pre_made, 1)

        def softplus(tile, stage):
            if stage == 0:
                wait(act, pre_made, tile.tiles(2, 2))
                wait(act, dt_made, tile.tiles(1, 0))
                nc.scalar.activation(spl[:, :, :], pre[:, :, :], ACT.Abs).then_inc(softplus_step, 1)
            elif stage == 1:
                wait(act, softplus_step, tile.tiles(3, 1))
                nc.scalar.activation(spl[:, :, :], spl[:, :, :], ACT.Exp, scale=-1.0).then_inc(softplus_step, 1)
            else:
                wait(act, softplus_step, tile.tiles(3, 2))
                nc.scalar.activation(spl[:, :, :], spl[:, :, :], ACT.Ln, bias=1.0).then_inc(softplus_step, 1)

        front = {3: (high,), 5: (middle, lambda t: add_bias(t, 0)), 7: (lambda t: add_bias(t, 1), low),
                 8: (lambda t: softplus(t, 0),), 9: (lambda t: softplus(t, 1),), 10: (lambda t: softplus(t, 2),)}

        def make_skip(tile):
            wait(act, u_loaded[tile.j], tile.loads())
            wait(act, y_stored[tile.j], tile.loads() - 16)
            for half in range(2):
                ins = nc.scalar.activation(yo[:, tile.j, half, :], u[:, tile.j, half, :], ACT.Copy,
                                           scale=Dk[:, tile.k, half:half + 1])
            ins.then_inc(skip_made, 1)

        def whole_front(tile):
            for piece in (high, middle, low):
                piece(tile)
            for half in range(2):
                add_bias(tile, half)
            for stage in range(3):
                softplus(tile, stage)

        def decay(tile, n):
            if n == 0:
                wait(act, dt_made, tile.tiles(1, 1))
            wait(act, scanned, tile.tiles(NS, n + 1 - NB))
            if tile.first():
                act.wait_ge(h_zeroed, 2 * tile.k + 2)
            seam_state = last_states(tile)[1]
            nc.scalar.activation(dBu[:, n % NU, SEAM:SEAM + 1], h[:, n, seam_state:seam_state + 1], ACT.Copy)
            for half in range(2):
                ins = nc.scalar.activation(halves(dA[:, n % NB, :])[:, half, :], dt[:, tile.j, half, :], ACT.Exp,
                                           scale=A[:, tile.k, half, n:n + 1])
            ins.then_inc(dA_made, 1)

        def copy_C(tile, n):
            wait(act, C_made, tile.tiles(NS, n + 1))
            wait(act, hC_made, tile.tiles(NS, n + 1 - NB))
            nc.scalar.activation(Cb[:, n % NB, :], C_ps[:, n % 2, :], ACT.Copy).then_inc(Cb_made, 1)

        def body(tile):
            for n in range(NS):
                if n + 1 < NS:
                    decay(tile, n + 1)
                copy_C(tile, n)
                for piece in front.get(n, ()) if tile.next() else ():
                    piece(tile.next())
                if n == 3:
                    make_skip(tile)
                if n == NS - 1 and tile.next():
                    decay(tile.next(), 0)

        whole_front(Tile(0, 0, 0))
        decay(Tile(0, 0, 0), 0)
        for_tiles(act, body)

    @block.vector
    def _(dve):
        def rest1(tile):
            wait(dve, high_made, tile.tiles(1, 1))
            wait(dve, low_made, tile.tiles(1, 0))
            nc.vector.tensor_tensor(rest[64:P, :], xd_ps[64:P, :], bc[64:P, tile.j, :], ALU.subtract)\
              .then_inc(rest1_made, 1)

        def rest2(tile):
            wait(dve, mid_made, tile.tiles(1, 1))
            nc.vector.tensor_tensor(rest[96:P, :], rest[96:P, :], bc[96:P, tile.j, :], ALU.subtract)\
              .then_inc(rest2_made, 1)

        def make_dt(tile):
            wait(dve, softplus_step, tile.tiles(3, 3))
            wait(dve, dA_made, tile.tiles(NS, -NS))
            nc.vector.scalar_tensor_tensor(out=dt[:, tile.j, :, :], in0=pre[:, :, :], scalar=0.0,
                                           in1=spl[:, :, :], op0=ALU.max, op1=ALU.add).then_inc(dt_made, 1)

        def make_dBu(tile, n):
            wait(dve, B_made, tile.tiles(NS, n + 1))
            wait(dve, scanned, tile.tiles(NS, n + 1 - NU))
            nc.vector.tensor_tensor(halves(dBu[:, n % NU, :]), du[:, tile.j, :, :], both(B_ps[:, n % 2, :]), ALU.mult)\
              .then_inc(dBu_made, 1)

        def finish_y(tile):
            wait(dve, y_summed, tile.tiles(NS, NS))
            wait(dve, skip_made, tile.tiles(1, 1))
            nc.vector.tensor_tensor(yo[:, tile.j, :, :], yo[:, tile.j, :, :], y_ps[:, :, :], ALU.add)\
              .then_inc(yo_made, 1)

        front = {4: rest1, 6: rest2, 11: make_dt}

        def body(tile):
            start = last_states(tile)[0]
            if tile.first():
                wait(dve, hC_made, tile.tiles(NS, 0))
                for state in last_states(tile):
                    nc.vector.memset(h[:, :, state:state + 1], 0.0).then_inc(h_zeroed, 1)
                dve.wait_ge(h_zeroed, 2 * tile.k + 2)
            for n in range(NS):
                if n + 1 < NS:
                    make_dBu(tile, n + 1)
                wait(dve, dA_made, tile.tiles(NS, n + 1))
                wait(dve, dBu_made, tile.tiles(NS, n + 1))
                wait(dve, hC_made, tile.tiles(NS, n + 1 - NS))
                nc.vector.tensor_tensor_scan(run(h[:, n, :], tile), run(dA[:, n % NB, :], tile),
                                             run(dBu[:, n % NU, :], tile), h[:, n, start:start + 1],
                                             ALU.mult, ALU.add).then_inc(scanned, 1)
                if n == 3 and tile.before():
                    finish_y(tile.before())
                if tile.next() and n in front:
                    front[n](tile.next())
                if n == NS - 1 and tile.next():
                    wait(dve, du_made, tile.next().tiles(1, 1))
                    make_dBu(tile.next(), 0)

        nc.vector.memset(dA[:, :, SEAM:SEAM + 1], 0.0).then_inc(seam_zeroed, 1)
        dve.wait_ge(seam_zeroed, 1)
        for piece in (rest1, rest2, make_dt):
            piece(Tile(0, 0, 0))
        dve.wait_ge(du_made, 1)
        make_dBu(Tile(0, 0, 0), 0)
        for_tiles(dve, body)
        finish_y(Tile(DIRS - 1, NT // 2 - 1, 1))

    @block.tensor
    def _(pe):
        pe.wait_ge(weights_loaded, WEIGHT_DMAS * 16)
        pe.wait_ge(selectors_built, 6)

        def project(tile, half):
            if half == 0:
                wait(pe, u_loaded[tile.j], tile.loads())
                wait(pe, high_made, tile.tiles(1, 0))
                wait(pe, rest1_made, tile.tiles(1, 0))
            ins = nc.tensor.matmul(xd_ps[:, :], xp[:, tile.k, half, :], u[:, tile.j, half, :],
                                   start=half == 0, stop=half == 1)
            if half == 1:
                ins.then_inc(xd_made, 1)

        def raw_dt(tile, half):
            wait(pe, high_made, tile.tiles(1, 1))
            wait(pe, pre_made, tile.tiles(2, half))
            nc.tensor.matmul(dt_ps[:, :], dtw[DT0:DT0 + R, tile.k, half, :], dts[DT0:DT0 + R, :],
                             start=True, stop=True).then_inc(dtraw_made, 1)

        def spread_B(tile, n):
            if n == 0:
                wait(pe, low_made, tile.tiles(1, 1))
            wait(pe, dBu_made, tile.tiles(NS, n - 1))
            nc.tensor.matmul(B_ps[:, n % 2, :], sel[:, n, :], bc[:, tile.j, :], start=True, stop=True)\
              .then_inc(B_made, 1)

        def spread_C(tile, n):
            wait(pe, Cb_made, tile.tiles(NS, n - 1))
            nc.tensor.matmul(C_ps[:, n % 2, :], sel[:, NS + n, :], bc[:, tile.j, :], start=True, stop=True)\
              .then_inc(C_made, 1)

        def add_before(tile, half):
            wait(pe, yp_loaded[tile.j], tile.loads() - NT * 16)
            nc.tensor.matmul(y_ps[:, half, :], ident[:, :], yp[:, tile.j, half, :], start=False, stop=False)

        def add_step(tile, n):
            if n == 0:
                wait(pe, yo_made, tile.tiles(1, 0))
            wait(pe, hC_made, tile.tiles(NS, n + 1))
            for half in range(2):
                ins = nc.tensor.matmul(y_ps[:, half, :], ident[:, :], hC[:, n % NB, half, :],
                                       start=n == 0, stop=n == NS - 1)
            ins.then_inc(y_summed, 1)

        def body(tile):
            for n in range(NS):
                if n + 2 < NS:
                    spread_B(tile, n + 2)
                elif tile.next():
                    spread_B(tile.next(), n + 2 - NS)
                if n + 1 < NS:
                    spread_C(tile, n + 1)
                elif tile.next():
                    spread_C(tile.next(), 0)
                if tile.next():
                    if n in (2, 3):
                        project(tile.next(), n - 2)
                    if n in (5, 7):
                        raw_dt(tile.next(), int(n == 7))
                if n in (10, 11) and tile.k >= 2:
                    add_before(tile, n - 10)
                if n >= LAG:
                    add_step(tile, n - LAG)
                elif tile.before():
                    add_step(tile.before(), n - LAG + NS)

        for half in range(2):
            project(Tile(0, 0, 0), half)
        for half in range(2):
            raw_dt(Tile(0, 0, 0), half)
        for n in range(2):
            spread_B(Tile(0, 0, 0), n)
        spread_C(Tile(0, 0, 0), 0)
        for_tiles(pe, body)
        for n in range(NS - LAG, NS):
            add_step(Tile(DIRS - 1, NT // 2 - 1, 1), n)


def output_phase(nc, es, w, x1_dram, mean, rstd, y_rows, y_columns, out):
    HALVES, ROWS = 2, 8
    CHUNKS, T = WIN // ROWS, ROWS * WIN
    Q = T // P
    sb = lambda name, shape: es.enter_context(nc.sbuf_tensor(f"ou_{name}", shape, F32))
    ps = lambda name, shape: es.enter_context(nc.psum_tensor(f"ou_{name}", shape, F32))
    sem = lambda name: es.semaphore(f"ou_{name}")
    pair = lambda name: [sem(f"{name}{b}") for b in range(2)]

    ident, mean_of = sb("ident", [P, P]), sb("mean_of", [P, P])
    wz, wout = sb("wz", [P, 2 * P]), sb("wout", [P, HALVES, C])
    ln_w, ln_b = sb("ln_w", [P, HALVES]), sb("ln_b", [P, HALVES])
    w_scaled, w_shift = sb("w_scaled", [P, HALVES, C]), sb("w_shift", [P, HALVES, C])
    yb = sb("yb", [P, 2, HALVES, WIN, WIN])
    ya, x1 = sb("ya", [P, 2, HALVES, T]), sb("x1", [P, 2, T])
    y, yc, sq = sb("y", [P, 2, HALVES, T]), sb("yc", [P, 2, HALVES, T]), sb("sq", [P, 2, HALVES, T])
    xn, sz, ysz = sb("xn", [P, 2, T]), sb("sz", [P, 2, HALVES, T]), sb("ysz", [P, 2, HALVES, T])
    var, r = sb("var", [P, 2, Q]), sb("r", [P, 2, Q])
    power = sb("power", [P, Q])
    scaled, res = sb("scaled", [P, 2, Q, C]), sb("res", [P, 2, Q, C])
    mean_ps, z_ps = ps("mean_ps", [P, T]), ps("z_ps", [P, HALVES, T])
    var_ps = ps("var_ps", [P, T])
    main_ps, side_ps = ps("main_ps", [P, 2, Q, C]), ps("side_ps", [P, 2, Q, C])

    built, w_loaded, w_made = sem("built"), sem("w_loaded"), sem("w_made")
    ya_loaded, yb_loaded, x1_loaded = map(pair, ("ya_loaded", "yb_loaded", "x1_loaded"))
    stored = [es.kept_semaphore(f"ou_stored{b}") for b in range(2)]
    y_made, mean_made, yc_made, sq_made, var_made, var_copied, r_made = map(
        pair, ("y_made", "mean_made", "yc_made", "sq_made", "var_made", "var_copied", "r_made"))
    xn_made, z_made, sz_made, ysz_made, main_made, side_made, scaled_made, res_made = map(
        pair, ("xn_made", "z_made", "sz_made", "ysz_made", "main_made", "side_made", "scaled_made", "res_made"))
    block = es.enter_context(nc.Block())

    class Chunk:
        def __init__(self, t, c):
            self.t, self.c, self.b = t, c, c % 2

        def turns(self, per=1, plus=0):
            return self.t.upto(CHUNKS // 2 * per, self.c // 2 * per + plus)

        def other(self):
            return self.t.upto(CHUNKS // 2, (self.c + 1) // 2)

    def for_chunks(eng, stages):
        most = max(lag for lag, _ in stages)

        def chunks_of(wy, v):
            return [Chunk(Window(wy, v, j), c) for j in range(2) for c in range(CHUNKS)]

        def step(chunks, s):
            for lag, stage in stages:
                if 0 <= s - lag < len(chunks):
                    stage(chunks[s - lag])

        def pair(wy, v):
            after = Window(wy, v, 1).next()
            chunks = chunks_of(wy, v) + (chunks_of(after.wy, after.v) if after else [])
            for s in range(2 * CHUNKS):
                step(chunks, s + most)

        for s in range(most):
            step(chunks_of(0, 0), s)
        for_window_pairs(eng, pair, last_alone=True)

    def halves(ap):
        return ap.unsqueeze(1).to_broadcast([P, HALVES, T])

    @block.sync
    def _(sp):
        sp.dma_start(wz[:, :], w["W_in"][:, 2 * P:4 * P]).then_inc(w_loaded, 16)
        sp.dma_start(wout[:, :, :], w["W_out"].rearrange("(s p) c -> p s c", s=HALVES)).then_inc(w_loaded, 16)
        sp.dma_start(ln_w[:, :], w["ln_w"]).then_inc(w_loaded, 16)
        sp.dma_start(ln_b[:, :], w["ln_b"]).then_inc(w_loaded, 16)

        def load_yb(t, c):
            if c == 0:
                wait(sp, y_made[1], t.upto(CHUNKS // 2, -CHUNKS // 2))
            half, width = c // (CHUNKS // 2), WIN // (CHUNKS // 2)
            x = c % (CHUNKS // 2) * width
            sp.dma_start(yb[:, t.j, half, x:x + width, :],
                         y_columns[half].rearrange("p (x y) -> p x y", y=N)
                         [:, bass.ds(t.wx(WIN) + x, width), bass.ds(t.wy * WIN, WIN)]).then_inc(yb_loaded[t.j], 16)

        def load(k):
            t, c, b = k.t, k.c, k.b
            y0, x0 = t.wy * WIN + c * ROWS, t.wx(WIN)
            wait(sp, y_made[b], k.turns())
            for half in range(HALVES):
                sp.dma_start(ya[:, b, half, :].rearrange("p (y x) -> p y x", x=WIN),
                             y_rows[half].rearrange("p (y x) -> p y x", x=N)
                             [:, bass.ds(y0, ROWS), bass.ds(x0, WIN)]).then_inc(ya_loaded[b], 16)
            wait(sp, side_made[b], k.turns())
            wait(sp, xn_made[b], k.turns())
            sp.dma_start(x1[:, b, :].rearrange("p (y x) -> p y x", x=WIN),
                         x1_dram[:, bass.ds(y0 + 1, ROWS), bass.ds(x0 + 1, WIN)]).then_inc(x1_loaded[b], 16)
            if t.next():
                load_yb(t.next(), c)

        for c in range(CHUNKS):
            load_yb(Window(0, 0, 0), c)
        for_chunks(sp, [(0, load)])

    @block.gpsimd
    def _(pool):
        build_identity(pool, nc, ident, built, 0)
        nc.gpsimd.memset(mean_of[:, :], 1.0 / (2 * P)).then_inc(built, 1)
        nc.gpsimd.memset(power[:, :], -0.5).then_inc(built, 1)
        pool.wait_ge(built, 4)

        def add_y(k):
            t, c, b = k.t, k.c, k.b
            if c == 0:
                wait(pool, yb_loaded[t.j], t.turns(CHUNKS * 16, CHUNKS * 16))
            wait(pool, ya_loaded[b], k.turns(HALVES * 16, HALVES * 16))
            wait(pool, mean_made[b], k.turns())
            wait(pool, yc_made[b], k.turns())
            for half in range(HALVES):
                ins = nc.gpsimd.tensor_tensor(
                    y[:, b, half, :].rearrange("p (y x) -> p y x", x=WIN),
                    ya[:, b, half, :].rearrange("p (y x) -> p y x", x=WIN),
                    yb[:, t.j, half, :, c * ROWS:(c + 1) * ROWS].rearrange("p x y -> p y x"), ALU.add)
            ins.then_inc(y_made[b], 1)

        def make_r(k):
            b = k.b
            wait(pool, var_copied[b], k.turns(1, 1))
            wait(pool, scaled_made[b], k.turns())
            nc.gpsimd.tensor_tensor(r[:, b, :], var[:, b, :], power[:, :], ALU.pow).then_inc(r_made[b], 1)

        def store(k):
            t, c, b = k.t, k.c, k.b
            wait(pool, res_made[b], k.turns(1, 1))
            for row in range(2):
                pool.dma_start(
                    out.rearrange("(y r) x c -> r x y c", r=2)
                    [row, bass.ds(t.wx(WIN), WIN), bass.ds(t.wy * (WIN // 2) + c * (ROWS // 2), Q), :],
                    res[row * WIN:(row + 1) * WIN, b, :, :]).then_inc(stored[b], 16)

        for_chunks(pool, [(0, add_y), (2, make_r), (3, store)])
        for b in range(2):
            pool.wait_ge(stored[b], SIDE * SIDE * CHUNKS // 2 * 2 * 16)

    @block.tensor
    def _(pe):
        pe.wait_ge(built, 4)
        pe.wait_ge(w_made, 4)

        def take_mean(k):
            b = k.b
            wait(pe, y_made[b], k.turns(1, 1))
            wait(pe, yc_made[1 - b], k.other())
            for half in range(HALVES):
                ins = nc.tensor.matmul(mean_ps[:, :], mean_of[:, :], y[:, b, half, :], start=half == 0, stop=half == 1)
            ins.then_inc(mean_made[b], 1)

        def take_z(k):
            b = k.b
            wait(pe, xn_made[b], k.turns(1, 1))
            wait(pe, sz_made[1 - b], k.other())
            for half in range(HALVES):
                ins = nc.tensor.matmul(z_ps[:, half, :], wz[:, half * P:(half + 1) * P], xn[:, b, :],
                                       start=True, stop=True)
            ins.then_inc(z_made[b], 1)

        def columns(ap, q):
            return ap[:, q * P:(q + 1) * P]

        def take_var(k):
            b = k.b
            wait(pe, sq_made[b], k.turns(1, 1))
            wait(pe, var_copied[1 - b], k.other())
            for q in range(Q):
                for half in range(HALVES):
                    ins = nc.tensor.matmul(var_ps[:, q:q + 1], columns(sq[:, b, half, :], q), mean_of[:, 0:1],
                                           start=half == 0, stop=half == 1)
            ins.then_inc(var_made[b], 1)

        def side(k):
            b = k.b
            wait(pe, sz_made[b], k.turns(1, 1))
            wait(pe, x1_loaded[b], k.turns(16, 16))
            wait(pe, res_made[b], k.turns())
            for q in range(Q):
                nc.tensor.matmul(side_ps[:, b, q, :], columns(x1[:, b, :], q), ident[:, :], start=True, stop=False)
                for half in range(HALVES):
                    ins = nc.tensor.matmul(side_ps[:, b, q, :], columns(sz[:, b, half, :], q), w_shift[:, half, :],
                                           start=False, stop=half == 1)
            ins.then_inc(side_made[b], 1)

        def main(k):
            b = k.b
            wait(pe, ysz_made[b], k.turns(1, 1))
            wait(pe, scaled_made[b], k.turns())
            for q in range(Q):
                for half in range(HALVES):
                    ins = nc.tensor.matmul(main_ps[:, b, q, :], columns(ysz[:, b, half, :], q), w_scaled[:, half, :],
                                           start=half == 0, stop=half == 1)
            ins.then_inc(main_made[b], 1)

        for_chunks(pe, [(0, take_z), (0, take_mean), (1, side), (1, take_var), (1, main)])

    @block.scalar
    def _(act):
        act.preload_act_table(ACT.Silu)

        def silu(k):
            b = k.b
            wait(act, z_made[b], k.turns(1, 1))
            wait(act, side_made[b], k.turns())
            wait(act, ysz_made[b], k.turns())
            nc.scalar.activation(sz[:, b, :, :], z_ps[:, :, :], ACT.Silu).then_inc(sz_made[b], 1)

        def square(k):
            b = k.b
            wait(act, yc_made[b], k.turns(1, 1))
            wait(act, var_made[b], k.turns())
            nc.scalar.activation(sq[:, b, :, :], yc[:, b, :, :], ACT.Square).then_inc(sq_made[b], 1)

        for_chunks(act, [(0, silu), (0, square)])

    @block.vector
    def _(dve):
        dve.wait_ge(w_loaded, 4 * 16)
        for half in range(HALVES):
            nc.vector.tensor_scalar(w_scaled[:, half, :], wout[:, half, :], ln_w[:, half:half + 1], None, ALU.mult)\
              .then_inc(w_made, 1)
            nc.vector.tensor_scalar(w_shift[:, half, :], wout[:, half, :], ln_b[:, half:half + 1], None, ALU.mult)\
              .then_inc(w_made, 1)

        def norm_x(k):
            b = k.b
            wait(dve, x1_loaded[b], k.turns(16, 16))
            wait(dve, z_made[b], k.turns())
            nc.vector.tensor_scalar(xn[:, b, :], x1[:, b, :], mean[:, :], rstd[:, :], ALU.subtract, ALU.mult)\
              .then_inc(xn_made[b], 1)

        def center(k):
            b = k.b
            wait(dve, mean_made[b], k.turns(1, 1))
            wait(dve, sq_made[b], k.turns())
            wait(dve, ysz_made[b], k.turns())
            nc.vector.tensor_tensor(yc[:, b, :, :], y[:, b, :, :], halves(mean_ps[:, :]), ALU.subtract)\
              .then_inc(yc_made[b], 1)

        def gate(k):
            b = k.b
            wait(dve, sz_made[b], k.turns(1, 1))
            wait(dve, yc_made[b], k.turns(1, 1))
            wait(dve, main_made[b], k.turns())
            nc.vector.tensor_tensor(ysz[:, b, :, :], yc[:, b, :, :], sz[:, b, :, :], ALU.mult).then_inc(ysz_made[b], 1)

        def copy_var(k):
            b = k.b
            wait(dve, var_made[b], k.turns(1, 1))
            wait(dve, r_made[b], k.turns())
            nc.vector.tensor_scalar(var[:, b, :], var_ps[:, 0:Q], LN_EPS, None, ALU.add).then_inc(var_copied[b], 1)

        def finish(k):
            b = k.b
            wait(dve, main_made[b], k.turns(1, 1))
            wait(dve, r_made[b], k.turns(1, 1))
            wait(dve, res_made[b], k.turns())
            nc.vector.tensor_tensor(scaled[:, b, :, :], main_ps[:, b, :, :],
                                    r[:, b, :].unsqueeze(2).to_broadcast([P, Q, C]), ALU.mult)\
              .then_inc(scaled_made[b], 1)
            wait(dve, side_made[b], k.turns(1, 1))
            wait(dve, scaled_made[b], k.turns(1, 1))
            wait(dve, stored[b], k.turns(2 * 16))
            nc.vector.tensor_tensor(res[:, b, :, :], scaled[:, b, :, :], side_ps[:, b, :, :], ALU.add)\
              .then_inc(res_made[b], 1)

        for_chunks(dve, [(0, norm_x), (1, center), (1, gate), (2, copy_var), (3, finish)])


def build_program(nc, x, w, out):
    dram = lambda name, shape: nc.dram_tensor(name, shape, F32, kind="Internal").ap()
    xT = dram("xT_scratch", (C, L))
    bias = dram("bias_scratch", (HEADS, L))
    x1 = dram("x1_scratch", (C, PAD, PAD))
    u = dram("u_scratch", (2, 2, P, L))
    y = dram("y_scratch", (4, 2, P, L))
    with ExitStack() as kept:
        sb = lambda name, shape: kept.enter_context(nc.sbuf_tensor(name, shape, F32))
        stats = sb("stats", [P, L // 512, 6])
        mean_x, rstd_x, mean_x1, rstd_x1 = (sb(name, [P, 1]) for name in ("mean_x", "rstd_x", "mean_x1", "rstd_x1"))
        run_phase(nc, kept, transpose_phase, x.rearrange("b y x c -> (b y x) c"), xT, stats)
        run_phase(nc, kept, norm_phase, stats, mean_x, rstd_x, "nx")
        run_phase(nc, kept, bias_phase, xT, mean_x, rstd_x, w["Wb"], bias)
        run_phase(nc, kept, attention_phase, w, xT, bias, mean_x, rstd_x, x1, stats)
        run_phase(nc, kept, norm_phase, stats, mean_x1, rstd_x1, "n1")
        run_phase(nc, kept, conv_phase, w, x1, mean_x1, rstd_x1, u)
        run_phase(nc, kept, scan_phase, w, u, y, L)
        run_phase(nc, kept, output_phase, w, x1, mean_x1, rstd_x1, y[2], y[3], out.rearrange("b y x c -> (b y) x c"))


def kernel(**inputs):
    import numpy as np
    import concourse.bacc as bacc
    from concourse import mybir as my
    from concourse.bass_utils import run_bass_kernel_spmd

    given = {name: np.asarray(a) for name, a in inputs.items()}
    conv = {name.removeprefix("L1_conv_"): a for name, a in given.items() if name.startswith("L1_conv_")}
    laid = {name: given["L0_conv_" + name] for name in ("Wq", "Wk", "Wv", "Wb", "Wo", "Wg")}
    laid |= {
        "W_in": conv["W_in"].T,
        "conv_w": conv["conv_w"].reshape(2 * P, 9).T.reshape(-1),
        "conv_b": conv["conv_b"].reshape(2, P).T,
        "x_proj": conv["x_proj_w"].transpose(0, 2, 1),
        "dt_w": conv["dt_proj_w"].transpose(2, 0, 1).reshape(8, 4, 2, P),
        "dt_b": conv["dt_proj_b"].reshape(4, 2, P).transpose(2, 0, 1),
        "D": conv["Ds"].reshape(4, 2, P).transpose(2, 0, 1),
        "A_log": conv["A_logs"].reshape(4, 2, P, 16).transpose(2, 0, 1, 3),
        "ln_w": conv["ln_w"].reshape(2, P).T,
        "ln_b": conv["ln_b"].reshape(2, P).T,
        "W_out": conv["W_out"].T,
    }
    arrays = {"in_x": np.ascontiguousarray(given["x"])}
    arrays |= {f"in_{name}": np.ascontiguousarray(a) for name, a in laid.items()}
    nc = bacc.Bacc("TRN2", target_bir_lowering=False, num_devices=1)
    aps = {name.removeprefix("in_"): nc.dram_tensor(name, a.shape, my.dt.from_np(a.dtype), kind="ExternalInput").ap()
           for name, a in arrays.items()}
    out = nc.dram_tensor("out_x", (1, N, N, C), my.dt.float32, kind="ExternalOutput").ap()
    build_program(nc, aps.pop("x"), aps, out)
    return run_bass_kernel_spmd(nc, [arrays], core_ids=[0]).results[0]["out_x"]
```
